# Optimizing a Trainium2 kernel written in Bass

```python
import numpy as np
import jax
import jax.numpy as jnp

def _softmax(x, axis=-1):
    return jax.nn.softmax(x, axis=axis)

def _gelu(x):
    return jax.nn.gelu(x, approximate=True)

def _silu(x):
    return jax.nn.silu(x)

def _sigmoid(x):
    return jax.nn.sigmoid(x)

def _layernorm(x, axis=-1, eps=1e-05):
    m = jnp.mean(x, axis=axis, keepdims=True)
    v = jnp.var(x, axis=axis, keepdims=True)
    return (x - m) / jnp.sqrt(v + eps)

def _scatter_add(tgt, idx, src, axis=0):
    return tgt.at[idx].add(src)

def _segment_sum(src, seg, n):
    return jax.ops.segment_sum(src, seg, n)
kernel_name = 'mk_adj_resnorm_d1_adj_r2_a68433'

def setup_inputs(seed: int=0):
    np.random.seed(seed)
    _w = jnp.asarray

    def _rec_inputs():
        import jax
        import jax.numpy as jnp
        _gk = jax.random.key(seed)
        x = 7.22e-05 + 1 * jax.random.normal(jax.random.fold_in(_gk, 1), (3327, 512), jnp.float32)
        _w = (1.0 + jnp.arange(3327, dtype=jnp.float32)) ** (-0.5)
        _w = _w / _w.mean()
        _pij = jnp.clip(0.00480914 * _w[:, None] * _w[None, :], 0.0, 1.0)
        _a = jax.random.uniform(jax.random.fold_in(_gk, 2), (3327, 3327)) < _pij
        adj = _a.astype(jnp.int32)
        return (x, adj)
    x, adj = _rec_inputs()

    def _L0_gnn_setup():
        import jax, jax.numpy as jnp
        import numpy as np
        N, D, O = (4096, 512, 512)
        key = jax.random.key(seed)
        ks = jax.random.split(key, 6)
        s = 1.0 / np.sqrt(D)
        x = jax.random.normal(ks[0], (N, D), dtype=jnp.float32)
        adj = jax.random.randint(ks[1], (N, N), 0, 2, dtype=jnp.int32)
        Wf = jax.random.normal(ks[2], (D, D), dtype=jnp.float32) * s
        Wg = jax.random.normal(ks[3], (D, D), dtype=jnp.float32) * s
        W = jax.random.normal(ks[4], (D, O), dtype=jnp.float32) * s
        bf = jnp.zeros((D,), dtype=jnp.float32)
        bg = jnp.zeros((D,), dtype=jnp.float32)
        bW = jnp.zeros((O,), dtype=jnp.float32)
        return {'x': x, 'adj': adj, 'Wf': Wf, 'bf': bf, 'Wg': Wg, 'bg': bg, 'W': W, 'bW': bW}
    _L0_gnn_all = _L0_gnn_setup()
    _L0_gnn_in = {k: v for k, v in _L0_gnn_all.items() if k in ('Wf', 'bf', 'Wg', 'bg', 'W', 'bW')}
    del _L0_gnn_all
    return {'x': x, 'adj': adj, 'L0_gnn_Wf': _L0_gnn_in['Wf'], 'L0_gnn_bf': _L0_gnn_in['bf'], 'L0_gnn_Wg': _L0_gnn_in['Wg'], 'L0_gnn_bg': _L0_gnn_in['bg'], 'L0_gnn_W': _L0_gnn_in['W'], 'L0_gnn_bW': _L0_gnn_in['bW']}

def reference(x, adj, L0_gnn_Wf, L0_gnn_bf, L0_gnn_Wg, L0_gnn_bg, L0_gnn_W, L0_gnn_bW):
    import jax
    import jax.numpy as jnp

    def _L0_gnn_ref(x, adj, Wf, bf, Wg, bg, W, bW):
        import jax, jax.numpy as jnp
        import numpy as np
        N, D, O = (4096, 512, 512)
        NEG = jnp.float32(-9000000000000000.0)
        f = x @ Wf + bf
        g = x @ Wg + bg
        e = jax.nn.relu(f @ g.T)
        scores = jnp.where(adj > 0, e, NEG)
        attention = jax.nn.softmax(scores, axis=1)
        x_W = x @ W + bW
        return attention @ x_W
    x = _layernorm(x + _L0_gnn_ref(x, adj, L0_gnn_Wf, L0_gnn_bf, L0_gnn_Wg, L0_gnn_bg, L0_gnn_W, L0_gnn_bW), axis=-1)
    return x

_drawn_inputs = setup_inputs


def setup_inputs(seed=0):
    import zlib

    import numpy as np

    out = dict(_drawn_inputs(seed))
    spreads = {'L0_gnn_bf': (0.0, 0.1), 'L0_gnn_bg': (0.0, 0.46), 'L0_gnn_bW': (0.0, 0.1)}
    factors = {}
    for name, (base, spread) in spreads.items():
        noise = np.random.default_rng([zlib.crc32(name.encode()), seed]).standard_normal(out[name].shape)
        drawn = base * np.exp(spread * noise) if base else spread * noise
        out[name] = jnp.asarray(drawn.astype(out[name].dtype))
    for name, factor in factors.items():
        out[name] = (out[name] * factor).astype(out[name].dtype)
    return out
```

```python
from contextlib import ExitStack

import concourse.bass as bass
from concourse import mybir

ALU = mybir.AluOpType
ACT = mybir.ActivationFunctionType
AX = mybir.AxisListType
F32 = mybir.dt.float32
F16 = mybir.dt.float16
BF16 = mybir.dt.bfloat16
I32 = mybir.dt.int32
RED_MAX = bass.bass_isa.ReduceOp.max

P = 128
BLOCK = 512
EPS = 1e-5
TOP = 14
PSCALE = float(2 ** TOP)
MASKED = -float(2.0 ** 126)
PADDED = -float(2.0 ** 127)
LEAST_MAX = float(2.0 ** -30)
EXPONENT_BITS = 0x7F800000
SCALE_BITS = float((TOP + 2 * 127) << 23)


def gnn_kernel(nc, x, adj, Wf, bf, Wg, bg, W, bW, out):
    N, D = x.shape
    KC = D // P
    T = (N + P - 1) // P
    NP = T * P
    LAST = N - (T - 1) * P
    L16 = LAST // 16 * 16
    NB = (NP + BLOCK - 1) // BLOCK
    widths = [min(BLOCK, NP - b * BLOCK) for b in range(NB)]
    real = [min(BLOCK, N - b * BLOCK) for b in range(NB)]
    JT = BLOCK // P
    assert D == BLOCK and KC == 4 and T % 2 == 0 and NP == N + 1
    PAIRS = T // 2

    with ExitStack() as ctx:
        def sb(name, shape, dt):
            return ctx.enter_context(nc.sbuf_tensor(name, shape, dt))

        def sem(name):
            return ctx.enter_context(nc.semaphore(name))

        xT = sb("xT", [P, 2, KC, NP], F16)
        V = sb("V", [P, T, 2, D], F16)
        x_nat = V[:, :, :, :].rearrange("p t s d -> p (t s d)").bitcast(F32).rearrange(
            "p (t d) -> p t d", t=T)
        A = sb("A", [P, KC, 2, D], F16)
        uT = sb("uT", [P, KC, 2, 2 * P], F16)
        ident = sb("ident", [P, P], F32)
        r_all = sb("r_all", [P, T], F32)
        S = sb("S", [P, 2, NP], F32)
        adj_t = sb("adj_t", [P, N], I32)
        carrier = sb("carrier", [P, NB + 1], F32)
        r_now = sb("r_now", [P, 2], F32)
        penalty = sb("penalty", [P, NP], BF16)
        relu_t = sb("relu_t", [P, 2, BLOCK], F32)
        PT = sb("PT", [P, 2, 2, BLOCK], F16)
        u32 = sb("u32", [P, KC, 2 * P], F32)
        x_res = sb("x_res", [P, D], F32)
        y = sb("y", [P, D], F32)
        o = sb("o", [P, D], F32)
        Wf_n = S[:, 0, 0:KC * D].rearrange("p (c d) -> p c d", c=KC)
        Wg_n = S[:, 1, 0:KC * D].rearrange("p (c d) -> p c d", c=KC)
        W_n = adj_t[:, 0:KC * D].bitcast(F32).rearrange("p (c d) -> p c d", c=KC)
        WfT = sb("WfT", [P, KC, D], F32)
        WgT = sb("WgT", [P, KC, D], F32)
        Ws = S[:, 0, 0:KC * D].bitcast(F16).rearrange("p (c s d) -> p c s d", c=KC, s=2)
        x_stage = u32[:, :, :].rearrange("p c n -> p (c n)").rearrange("p (b d) -> p b d", b=2)
        v32 = S[:, 1, 0:2 * D].rearrange("p (b d) -> p b d", b=2)
        bWs = y
        bf_c = sb("bf_c", [P, KC], F32)
        bg_c = sb("bg_c", [P, KC], F32)
        bb_c = sb("bb_c", [P, KC], F32)
        ones = sb("ones", [P, P], F32)
        c_col = sb("c_col", [P, KC], F32)
        cs_col = sb("cs_col", [P, KC], F32)
        wr32 = sb("wr32", [P, KC], F32)
        wr = sb("wr", [P, KC, 2], F16)
        r_part = sb("r_part", [P, T, 2], F32)
        xmax = sb("xmax", [P, 8], F32)
        stats = sb("stats", [P, 8], F32)
        stats_all = sb("stats_all", [P, 8], F32)
        sc = sb("sc", [P, 40], F32)
        row_max = sb("row_max", [P, 2, NB], F32)
        max_all = sb("max_all", [P, 2], F32)
        nbias = sb("nbias", [P, 2], F32)
        row_sum = sb("row_sum", [P, 2, NB], F32)
        fin = sb("fin", [P, 8], F32)
        bn6 = sb("bn6", [P, 6], F32)
        bn2 = sb("bn2", [P, 2], F32)
        neg_half = sb("neg_half", [P, 1], F32)

        ps = ctx.enter_context(nc.psum_tensor("ps", [P, 8, BLOCK], F32))
        S_BANK, PT_BANK, O_BANK, U_BANK, C_SMALL, A_BANK = 0, 2, 4, 5, 0, 4

        weights_in = sem("weights_in")
        w_in = sem("w_in")
        biases_in = sem("biases_in")
        bW_in = sem("bW_in")
        x_in = [sem(f"x_in{n}") for n in range(6)]
        pad_zeroed = sem("pad_zeroed")
        ident_zeroed = sem("ident_zeroed")
        ident_ready = sem("ident_ready")
        ones_ready = sem("ones_ready")
        half_ready = sem("half_ready")
        wt_done = sem("wt_done")
        wf_copied = sem("wf_copied")
        wg_copied = sem("wg_copied")
        a_done = sem("a_done")
        bb_ready = sem("bb_ready")
        prep = sem("prep")
        stats_ready = sem("stats_ready")
        stats_summed = sem("stats_summed")
        scales_ready = sem("scales_ready")
        split_hi = sem("split_hi")
        split_ready = sem("split_ready")
        staged = sem("staged")
        xt_done = sem("xt_done")
        xt_hi = sem("xt_hi")
        xt_lo = sem("xt_lo")
        v_done = sem("v_done")
        v_f32 = sem("v_f32")
        v_hi = sem("v_hi")
        v_lo = sem("v_lo")
        r_copied = sem("r_copied")
        r_ready = sem("r_ready")
        u_done = sem("u_done")
        u_f32 = sem("u_f32")
        u_hi = sem("u_hi")
        u_ready = sem("u_ready")
        adj_in = sem("adj_in")
        penalty_ready = sem("penalty_ready")
        r_now_ready = sem("r_now_ready")
        scores_done = sem("scores_done")
        relu_done = sem("relu_done")
        masked = sem("masked")
        max_ready = sem("max_ready")
        bias_ready = sem("bias_ready")
        exp_done = sem("exp_done")
        pt_done = sem("pt_done")
        pt_hi = sem("pt_hi")
        pt_lo = sem("pt_lo")
        av_done = sem("av_done")
        x_res_in = sem("x_res_in")
        norm = sem("norm")
        rstd_ready = sem("rstd_ready")
        out_ready = sem("out_ready")
        stored = sem("stored")
        y_ready = sem("y_ready")

        (mA, mW, mX, mU, mV, sA, sW, sX, sU, sV, t0, t1, unit_AX, unit_WX, iAX, iWX, ratio_u, ratio_v,
         iA, ratio_r, UX, score_unit, beta, iV, out_unit, neg_unit) = range(26)

        def col(k, n=1):
            return sc[:, k:k + n]

        def load_rows(eng, dst, src, tile, rows, signal):
            cut = 64 if rows == P else L16
            eng.dma_start(dst[0:cut], src[bass.ds(tile * P, cut)] if not isinstance(tile, int)
                          else src[tile * P:tile * P + cut]).then_inc(signal, 16)
            eng.dma_start(dst[cut:rows], src[bass.ds(tile * P + cut, rows - cut)] if not isinstance(tile, int)
                          else src[tile * P + cut:tile * P + rows]).then_inc(signal, 16)

        def cols(ap, start, n):
            return ap[:, bass.ds(start, n)] if not isinstance(start, int) else ap[:, start:start + n]

        def x_at(t):
            return x_nat[:, t, :] if isinstance(t, int) else x_nat[:, bass.ds(t, 1), :].squeeze(1)

        def V_at(t, half):
            return V[:, t, half, :] if isinstance(t, int) else V[:, bass.ds(t, 1), half, :].squeeze(1)

        def xT_at(t, half):
            return xT[:, half, :, t * P:(t + 1) * P] if isinstance(t, int) else xT[:, half, :, bass.ds(t * P, P)]

        def x_chunk(t, half, k):
            return (xT[:, half, k, t * P:(t + 1) * P] if isinstance(t, int)
                    else xT[:, half, k, bass.ds(t * P, P)])

        def wait_apart(dve, signal, value, word):
            dve.wait_ge(signal, value)
            nc.vector.memset(carrier[:, word:word + 1], 0.0)

        block = ctx.enter_context(nc.Block())

        @block.sync
        def _(sp):
            for n in range(5):
                sp.dma_start(x_nat[:, 5 * n:5 * n + 5, :],
                             x[5 * n * P:(5 * n + 5) * P, :].rearrange("(t p) d -> p t d", p=P)).then_inc(x_in[n], 16)
            sp.wait_ge(pad_zeroed, 1)
            sp.dma_start(x_nat[0:L16, T - 1, :], x[(T - 1) * P:(T - 1) * P + L16, :]).then_inc(x_in[5], 16)
            sp.dma_start(x_nat[L16:LAST, T - 1, :], x[(T - 1) * P + L16:N, :]).then_inc(x_in[5], 16)
            sp.wait_ge(split_ready, 3)
            load_rows(sp, adj_t, adj, 0, P, adj_in)
            sp.wait_ge(penalty_ready, 1)
            load_rows(sp, adj_t, adj, 1, P, adj_in)
            load_rows(sp, x_res, x, 0, P, x_res_in)

            def step(i, adj_rows, x_rows):
                if adj_rows:
                    sp.wait_ge(penalty_ready, i + 1)
                    load_rows(sp, adj_t, adj, i + 1, adj_rows, adj_in)
                sp.wait_ge(out_ready, i)
                rows = P
                cut = 64
                for a, b in ((0, cut), (cut, rows)):
                    dst = (out[bass.ds((i - 1) * P + a, b - a)] if not isinstance(i, int)
                           else out[(i - 1) * P + a:(i - 1) * P + b])
                    sp.dma_start(dst, o[a:b]).then_inc(stored, 16)
                load_rows(sp, x_res, x, i, x_rows, x_res_in)

            step(1, P, P)
            with sp.Fori(0, PAIRS - 2) as p:
                step(p * 2 + 2, P, P)
                step(p * 2 + 3, P, P)
            step(T - 2, LAST, P)
            step(T - 1, 0, LAST)
            sp.wait_ge(out_ready, T)
            for a, b in ((0, L16), (L16, LAST)):
                sp.dma_start(out[(T - 1) * P + a:(T - 1) * P + b], o[a:b]).then_inc(stored, 16)
            sp.wait_ge(stored, 32 * T)

        @block.gpsimd
        def _(pool):
            nc.gpsimd.memset(ident[:, :], 0.0).then_inc(ident_zeroed, 1)
            pool.wait_ge(ident_zeroed, 1)
            nc.gpsimd.affine_select(out=ident[:, :], in_=ident[:, :], compare_op=ALU.not_equal, fill=1.0, base=0,
                                    pattern=[[-1, P]], channel_multiplier=1).then_inc(ident_ready, 1)
            nc.gpsimd.memset(neg_half[:, :], -0.5).then_inc(half_ready, 1)
            pool.wait_ge(half_ready, 1)
            pool.wait_ge(stats_ready, 1)
            nc.gpsimd.partition_all_reduce(stats_all[:, 0:5], stats[:, 0:5], P, RED_MAX).then_inc(stats_summed, 1)
            pool.wait_ge(stats_ready, 2)
            nc.gpsimd.partition_all_reduce(stats_all[:, 5:6], stats[:, 5:6], P, RED_MAX).then_inc(stats_summed, 1)

            def step(i):
                pool.wait_ge(norm, i * 6)
                nc.gpsimd.tensor_tensor(fin[:, 5:6], fin[:, 4:5], neg_half[:, :], ALU.pow).then_inc(rstd_ready, 1)

            with pool.Fori(0, PAIRS) as p:
                step(p * 2 + 1)
                step(p * 2 + 2)

        @block.scalar
        def _(act):
            act.dma_start(Wf_n, Wf.rearrange("(c p) d -> p c d", p=P)).then_inc(weights_in, 16)
            act.dma_start(Wg_n, Wg.rearrange("(c p) d -> p c d", p=P)).then_inc(weights_in, 16)
            act.dma_start(W_n, W.rearrange("(c p) d -> p c d", p=P)).then_inc(w_in, 16)
            with nc.allow_non_contiguous_dma(reason="two vectors of 512 as columns"):
                act.dma_start(bf_c[:, :], bf.rearrange("(c p) -> p c", p=P)).then_inc(biases_in, 16)
                act.dma_start(bg_c[:, :], bg.rearrange("(c p) -> p c", p=P)).then_inc(biases_in, 16)
            act.dma_start(bWs[:, :], bW.rearrange("(a d) -> a d", a=1).to_broadcast([P, D])).then_inc(bW_in, 16)
            for c in range(KC):
                act.wait_ge(wt_done, 2 * c + 1)
                nc.scalar.copy(WfT[:, :, c * P:(c + 1) * P],
                               ps[:, 2 * (c % 2), :].rearrange("p (k n) -> p k n", k=KC)).then_inc(wf_copied, 1)
            act.wait_ge(scales_ready, 1)
            for c in range(KC):
                nc.scalar.activation(A[:, c, 0, :], ps[:, A_BANK + c, :], ACT.Copy, scale=col(sA)).then_inc(split_hi, 1)
            nc.scalar.activation(Ws[:, :, 0, :], W_n, ACT.Copy, scale=col(sW)).then_inc(split_hi, 1)

            def stage(t, h):
                if not (isinstance(t, int) and t < 2):
                    act.wait_ge(xt_done, t - 1)
                nc.scalar.activation(x_stage[:, h, :], x_at(t), ACT.Copy, scale=col(sX)).then_inc(staged, 1)

            def x_hi(t, h):
                act.wait_ge(xt_done, t + 1)
                nc.scalar.copy(xT_at(t, 0), ps[:, PT_BANK + h, :].rearrange("p (k n) -> p k n", k=KC)).then_inc(xt_hi, 1)

            def v_split(t, h):
                act.wait_ge(v_f32, t + 1)
                nc.scalar.copy(V_at(t, 0), v32[:, h, :]).then_inc(v_hi, 1)

            act.wait_ge(scales_ready, 2)
            stage(0, 0)
            x_hi(0, 0)
            stage(1, 1)

            def x_and_v(t):
                x_hi(t + 1, 1)
                stage(t + 2, 0)
                v_split(t, 0)
                x_hi(t + 2, 0)
                stage(t + 3, 1)
                v_split(t + 1, 1)

            x_and_v(0)
            with act.Fori(1, PAIRS - 1) as q:
                x_and_v(q * 2)
            x_hi(T - 1, 1)
            v_split(T - 2, 0)
            v_split(T - 1, 1)

            def u_split(pair):
                act.wait_ge(u_done, pair + 1)
                if not (isinstance(pair, int) and pair < 1):
                    act.wait_ge(u_ready, pair)
                for m in range(KC):
                    last = nc.scalar.activation(u32[:, m, :], ps[:, U_BANK + m // 2, (m % 2) * 2 * P:(m % 2 + 1) * 2 * P],
                                                ACT.Identity, bias=cs_col[:, m:m + 1], scale=col(ratio_u))
                last.then_inc(u_f32, 1)
                act.wait_ge(u_f32, pair + 1)
                nc.scalar.copy(uT[:, :, 0, :], u32[:, :, :]).then_inc(u_hi, 1)

            def relu(i, par, b):
                n = i * NB + b
                w = widths[b]
                if b == 0:
                    nc.scalar.copy(r_now[:, par:par + 1], cols(r_all, i, 1)).then_inc(r_now_ready, 1)
                    act.wait_ge(r_now_ready, i + 1)
                act.wait_ge(scores_done, n + 1)
                if not (isinstance(n, int) and n < 2):
                    act.wait_ge(masked, n - 1)
                nc.scalar.activation(relu_t[:, (par + b) % 2, 0:w], ps[:, S_BANK + (par + b) % 2, 0:w], ACT.Relu,
                                     bias=r_now[:, par:par + 1]).then_inc(relu_done, 1)

            def exp(i, par, b):
                if b == 0:
                    act.wait_ge(bias_ready, i + 1)
                w = widths[b]
                a = S[:, par, b * BLOCK:b * BLOCK + w]
                nc.scalar.activation(a, a, ACT.Exp, bias=nbias[:, par:par + 1], scale=col(score_unit),
                                     accum_out=row_sum[:, par, b:b + 1]).then_inc(exp_done, 1)

            def p_hi(i, par, b):
                n = i * NB + b
                w = widths[b]
                act.wait_ge(pt_done, n + 1)
                if not (isinstance(n, int) and n < 2):
                    act.wait_ge(av_done, n - 1)
                nc.scalar.activation(PT[:, (par + b) % 2, 0, 0:w], ps[:, PT_BANK + (par + b) % 2, 0:w], ACT.Copy,
                                     scale=PSCALE).then_inc(pt_hi, 1)

            def step(i, par, pair):
                for b in range(NB):
                    if b == NB - 2:
                        p_hi(i - 1, 1 - par, 0)
                    relu(i, par, b)
                p_hi(i - 1, 1 - par, 1)
                exp(i, par, 0)
                if pair is not None:
                    exp(i, par, 1)
                    exp(i, par, 2)
                    u_split(pair)
                for b in range(2, NB):
                    p_hi(i - 1, 1 - par, b)
                    if pair is None:
                        exp(i, par, b - 1)
                    elif b + 1 < NB:
                        exp(i, par, b + 1)
                if pair is None:
                    exp(i, par, NB - 1)

            act.wait_ge(r_ready, 1)
            u_split(0)
            for b in range(NB):
                relu(0, 0, b)
            for b in range(NB):
                exp(0, 0, b)
            step(1, 1, 1)
            with act.Fori(0, PAIRS - 2) as p:
                step(p * 2 + 2, 0, None)
                step(p * 2 + 3, 1, p + 2)
            step(T - 2, 0, None)
            step(T - 1, 1, None)
            for b in range(NB):
                p_hi(T - 1, 1, b)

        @block.vector
        def _(dve):
            done = [0]

            def link(ins):
                done[0] += 1
                ins.then_inc(prep, 1)
                dve.wait_ge(prep, done[0])

            def amax(dst, src):
                return nc.vector.tensor_reduce(dst, src, AX.X if len(src.shape) == 2 else AX.XY, ALU.max,
                                               apply_absolute_value=True)

            nc.vector.memset(x_nat[96:P, T - 1, :], 0.0).then_inc(pad_zeroed, 1)
            nc.vector.memset(ones[:, :], 1.0).then_inc(ones_ready, 1)
            nc.vector.memset(penalty[:, N:NP], PADDED)
            nc.vector.memset(stats[:, :], 0.0)
            dve.wait_ge(biases_in, 32)
            nc.vector.tensor_tensor(bb_c[:, :], bf_c[:, :], bg_c[:, :], ALU.mult).then_inc(bb_ready, 1)
            for c in range(KC):
                dve.wait_ge(wt_done, 2 * c + 2)
                nc.vector.tensor_copy(WgT[:, :, c * P:(c + 1) * P],
                                      ps[:, 2 * (c % 2) + 1, :].rearrange("p (k n) -> p k n", k=KC)).then_inc(wg_copied, 1)
            dve.wait_ge(w_in, 16)
            amax(stats[:, 1:2], W_n)
            dve.wait_ge(bW_in, 16)
            amax(stats[:, 2:3], bWs[:, :])
            dve.wait_ge(a_done, 1)
            amax(sc[:, 30:31], ps[:, A_BANK:A_BANK + KC, :])
            amax(sc[:, 31:32], ps[:, C_SMALL, KC:2 * KC])
            amax(stats[:, 3:4], ps[:, C_SMALL, 0:KC])
            nc.vector.tensor_copy(c_col[:, :], ps[:, C_SMALL, 0:KC])
            nc.vector.tensor_copy(wr32[:, :], ps[:, C_SMALL, KC:2 * KC])
            link(nc.vector.tensor_copy(col(beta), ps[:, C_SMALL, 2 * KC:2 * KC + 1]))
            nc.vector.tensor_tensor(stats[:, 0:1], sc[:, 30:31], sc[:, 31:32], ALU.max).then_inc(stats_ready, 1)

            def scale_of(dst, maximum, n):
                link(nc.vector.tensor_scalar(col(t0, n), maximum, LEAST_MAX, None, ALU.max))
                link(nc.vector.tensor_scalar(col(t0, n).bitcast(I32), col(t0, n).bitcast(I32), EXPONENT_BITS, None,
                                             ALU.bitwise_and))
                return nc.vector.tensor_scalar(dst.bitcast(I32), col(t0, n).bitcast(I32), -1.0, SCALE_BITS,
                                               ALU.mult, ALU.add)

            dve.wait_ge(stats_summed, 1)
            link(nc.vector.tensor_scalar(col(mA, 2), stats_all[:, 0:2], LEAST_MAX, None, ALU.max))
            last = scale_of(col(sA, 2), col(mA, 2), 2)
            last.then_inc(scales_ready, 1)
            for c in range(KC):
                dve.wait_ge(split_hi, c + 1)
                last = nc.vector.scalar_tensor_tensor(A[:, c, 1, :], ps[:, A_BANK + c, :], col(sA), A[:, c, 0, :],
                                                      ALU.mult, ALU.subtract)
            last.then_inc(split_ready, 1)
            link(nc.vector.tensor_scalar(wr32[:, :], wr32[:, :], col(sA), None, ALU.mult))
            link(nc.vector.tensor_copy(wr[:, :, 0], wr32[:, :]))
            nc.vector.tensor_tensor(wr[:, :, 1], wr32[:, :], wr[:, :, 0], ALU.subtract).then_inc(split_ready, 1)
            dve.wait_ge(split_hi, KC + 1)
            nc.vector.scalar_tensor_tensor(Ws[:, :, 1, :], W_n, col(sW), Ws[:, :, 0, :], ALU.mult,
                                           ALU.subtract).then_inc(split_ready, 1)
            for n in range(5):
                dve.wait_ge(x_in[n], 16)
                amax(xmax[:, n:n + 1], x_nat[:, 5 * n:5 * n + 5, :])
            dve.wait_ge(x_in[5], 32)
            link(amax(xmax[:, 5:6], x_nat[:, T - 1, :]))
            nc.vector.tensor_reduce(stats[:, 5:6], xmax[:, 0:6], AX.X, ALU.max).then_inc(stats_ready, 1)
            dve.wait_ge(stats_summed, 2)
            link(nc.vector.tensor_scalar(col(mX), stats_all[:, 5:6], LEAST_MAX, None, ALU.max))
            link(scale_of(col(sX), col(mX), 1))
            link(nc.vector.tensor_scalar(col(mU, 2), col(mA, 2), col(mX), float(D), ALU.mult, ALU.mult))
            nc.vector.tensor_tensor(col(mV), col(mV), stats_all[:, 2:3], ALU.add)
            link(nc.vector.tensor_tensor(col(mU), col(mU), stats_all[:, 3:4], ALU.add))
            link(scale_of(col(sU, 2), col(mU, 2), 2))
            link(nc.vector.tensor_scalar(col(unit_AX, 2), col(sA, 2), col(sX), None, ALU.mult))
            link(nc.vector.reciprocal(col(iAX, 2), col(unit_AX, 2)))
            link(nc.vector.reciprocal(col(iA), col(sA)))
            link(nc.vector.tensor_tensor(col(ratio_u, 2), col(iAX, 2), col(sU, 2), ALU.mult))
            nc.vector.tensor_scalar(bWs[:, :], bWs[:, :], col(sV), None, ALU.mult)
            nc.vector.tensor_scalar(cs_col[:, :], c_col[:, :], col(sU), None, ALU.mult)
            nc.vector.tensor_tensor(col(ratio_r), col(sU), col(iA), ALU.mult)
            link(nc.vector.tensor_tensor(col(UX), col(sU), col(sX), ALU.mult))
            link(nc.vector.reciprocal(col(score_unit), col(UX)))
            link(nc.vector.tensor_tensor(col(beta), col(beta), col(UX), ALU.mult))
            link(nc.vector.tensor_scalar(col(neg_unit), col(score_unit), -1.0, None, ALU.mult))
            link(nc.vector.reciprocal(col(iV), col(sV)))
            nc.vector.tensor_scalar(col(out_unit), col(iV), 1.0 / PSCALE, None, ALU.mult).then_inc(scales_ready, 1)

            def x_lo(t, h):
                dve.wait_ge(xt_hi, t + 1)
                nc.vector.tensor_tensor(xT_at(t, 1), ps[:, PT_BANK + h, :].rearrange("p (k n) -> p k n", k=KC),
                                        xT_at(t, 0), ALU.subtract).then_inc(xt_lo, 1)

            def v_from(t, h):
                dve.wait_ge(v_done, t + 1)
                if not (isinstance(t, int) and t < 2):
                    dve.wait_ge(v_hi, t - 1)
                dve.wait_ge(staged, t + 1)
                nc.vector.scalar_tensor_tensor(v32[:, h, :], ps[:, S_BANK + h, :], col(ratio_v), bWs[:, :], ALU.mult,
                                               ALU.add).then_inc(v_f32, 1)
                r_dst = r_part[:, t, :] if isinstance(t, int) else r_part[:, bass.ds(t, 1), :].squeeze(1)
                nc.vector.tensor_copy(r_dst, ps[:, O_BANK + h, 0:2]).then_inc(r_copied, 1)

            def v_lo_part(t, h):
                dve.wait_ge(v_hi, t + 1)
                nc.vector.tensor_tensor(V_at(t, 1), v32[:, h, :], V_at(t, 0), ALU.subtract).then_inc(v_lo, 1)

            x_lo(0, 0)

            def x_and_v(t):
                x_lo(t + 1, 1)
                v_from(t, 0)
                x_lo(t + 2, 0)
                v_lo_part(t, 0)
                v_from(t + 1, 1)
                v_lo_part(t + 1, 1)

            x_and_v(0)
            with dve.Fori(1, PAIRS - 1) as q:
                x_and_v(q * 2)
            x_lo(T - 1, 1)
            v_from(T - 2, 0)
            v_lo_part(T - 2, 0)
            v_from(T - 1, 1)
            v_lo_part(T - 1, 1)
            dve.wait_ge(r_copied, T)
            link(nc.vector.tensor_tensor(r_all[:, :], r_part[:, :, 0], r_part[:, :, 1], ALU.add))
            nc.vector.tensor_scalar(r_all[:, :], r_all[:, :], col(ratio_r), col(beta), ALU.mult,
                                    ALU.add).then_inc(r_ready, 1)

            def make_penalty(i, b, last=False):
                if b == 0:
                    dve.wait_ge(adj_in, i * 32 + 32)
                a = slice(b * BLOCK, b * BLOCK + real[b])
                ins = nc.vector.tensor_scalar(penalty[:, a], adj_t[:, a], 0.0, MASKED, ALU.is_le, ALU.mult)
                if b == NB - 1:
                    ins.then_inc(penalty_ready, 1)

            def mask(i, par, b):
                n = i * NB + b
                w = widths[b]
                if b == 0:
                    dve.wait_ge(penalty_ready, i + 1)
                    if not (isinstance(i, int) and i < 2):
                        dve.wait_ge(pt_done, (i - 1) * NB)
                wait_apart(dve, relu_done, n + 1, b)
                nc.vector.tensor_tensor_reduce(S[:, par, b * BLOCK:b * BLOCK + w], relu_t[:, (par + b) % 2, 0:w],
                                               penalty[:, b * BLOCK:b * BLOCK + w], 1.0, -3.0e38, ALU.add, ALU.max,
                                               row_max[:, par, b:b + 1]).then_inc(masked, 1)

            def make_bias(i, par):
                dve.wait_ge(masked, (i + 1) * NB)
                nc.vector.tensor_reduce(max_all[:, par:par + 1], row_max[:, par, :], AX.X, ALU.max).then_inc(max_ready, 1)
                dve.wait_ge(max_ready, i + 1)
                nc.vector.tensor_scalar(nbias[:, par:par + 1], max_all[:, par:par + 1], col(neg_unit), None,
                                        ALU.mult).then_inc(bias_ready, 1)

            def p_lo(i, par, b):
                n = i * NB + b
                w = widths[b]
                dve.wait_ge(pt_hi, n + 1)
                nc.vector.scalar_tensor_tensor(PT[:, (par + b) % 2, 1, 0:w], ps[:, PT_BANK + (par + b) % 2, 0:w],
                                               PSCALE, PT[:, (par + b) % 2, 0, 0:w], ALU.mult,
                                               ALU.subtract).then_inc(pt_lo, 1)

            def u_lo(pair):
                dve.wait_ge(u_hi, pair + 1)
                nc.vector.tensor_tensor(uT[:, :, 1, :], u32[:, :, :], uT[:, :, 0, :], ALU.subtract).then_inc(u_ready, 1)

            def finish(t, par):
                k = t * 6
                dve.wait_ge(exp_done, t * NB + NB)
                nc.vector.tensor_reduce(fin[:, 0:1], row_sum[:, par, :], AX.X, ALU.add).then_inc(norm, 1)
                dve.wait_ge(norm, k + 1)
                nc.vector.reciprocal(fin[:, 1:2], fin[:, 0:1]).then_inc(norm, 1)
                dve.wait_ge(norm, k + 2)
                nc.vector.tensor_scalar(fin[:, 2:3], fin[:, 1:2], col(out_unit), None, ALU.mult).then_inc(norm, 1)
                dve.wait_ge(norm, k + 3)
                dve.wait_ge(av_done, t * NB + NB)
                dve.wait_ge(x_res_in, t * 32 + 32)
                nc.vector.scalar_tensor_tensor(y[:, :], ps[:, O_BANK, :], fin[:, 2:3], x_res[:, :], ALU.mult,
                                               ALU.add).then_inc(y_ready, 1)
                dve.wait_ge(y_ready, t + 1)
                nc.vector.bn_stats(bn6[:, :], y[:, :]).then_inc(norm, 1)
                wait_apart(dve, norm, k + 4, NB)
                nc.vector.bn_aggr(bn2[:, :], bn6[:, :]).then_inc(norm, 1)
                dve.wait_ge(norm, k + 5)
                nc.vector.tensor_scalar(fin[:, 4:5], bn2[:, 1:2], EPS, None, ALU.add).then_inc(norm, 1)
                if not (isinstance(t, int) and t < 1):
                    dve.wait_ge(stored, t * 32)
                dve.wait_ge(rstd_ready, t + 1)
                nc.vector.tensor_scalar(o[:, :], y[:, :], bn2[:, 0:1], fin[:, 5:6], ALU.subtract,
                                        ALU.mult).then_inc(out_ready, 1)

            def step(i, par, pair, more):
                for b in range(NB):
                    if b == NB - 2:
                        p_lo(i - 1, 1 - par, 0)
                    mask(i, par, b)
                make_bias(i, par)
                p_lo(i - 1, 1 - par, 1)
                if more:
                    make_penalty(i + 1, 0)
                    make_penalty(i + 1, 1)
                if pair is not None:
                    u_lo(pair)
                for b in range(2, NB):
                    p_lo(i - 1, 1 - par, b)
                    if more:
                        make_penalty(i + 1, b)
                finish(i - 1, 1 - par)

            for b in range(NB):
                make_penalty(0, b)
            u_lo(0)
            for b in range(NB):
                mask(0, 0, b)
            make_bias(0, 0)
            for b in range(NB):
                make_penalty(1, b)
            step(1, 1, 1, True)
            with dve.Fori(0, PAIRS - 2) as p:
                step(p * 2 + 2, 0, None, True)
                step(p * 2 + 3, 1, p + 2, True)
            step(T - 2, 0, None, True)
            step(T - 1, 1, None, False)
            for b in range(NB):
                p_lo(T - 1, 1, b)
            finish(T - 1, 1)

        @block.tensor
        def _(pe):
            pe.wait_ge(ident_ready, 1)
            pe.wait_ge(weights_in, 32)
            for c in range(KC):
                if c >= 2:
                    pe.wait_ge(wf_copied, c - 1)
                    pe.wait_ge(wg_copied, c - 1)
                for s, w in enumerate((Wf_n, Wg_n)):
                    for k in range(KC):
                        last = nc.tensor.transpose(ps[:, 2 * (c % 2) + s, k * P:(k + 1) * P], w[:, c, k * P:(k + 1) * P],
                                                   ident[:, :])
                    last.then_inc(wt_done, 1)
            pe.wait_ge(wf_copied, KC)
            pe.wait_ge(wg_copied, KC)
            for m in range(KC):
                for k in range(KC):
                    nc.tensor.matmul(ps[:, A_BANK + m, :], WfT[:, k, m * P:(m + 1) * P], WgT[:, k, :], start=(k == 0),
                                     stop=(k == KC - 1))
            pe.wait_ge(biases_in, 32)
            pe.wait_ge(bb_ready, 1)
            pe.wait_ge(ones_ready, 1)
            for s, (w, b) in enumerate(((WgT, bf_c), (WfT, bg_c))):
                for m in range(KC):
                    for k in range(KC):
                        nc.tensor.matmul(ps[:, C_SMALL, s * KC + m:s * KC + m + 1], w[:, k, m * P:(m + 1) * P],
                                         b[:, k:k + 1], start=(k == 0), stop=(k == KC - 1))
            for k in range(KC):
                last = nc.tensor.matmul(ps[:, C_SMALL, 2 * KC:2 * KC + 1], ones[:, :], bb_c[:, k:k + 1],
                                        start=(k == 0), stop=(k == KC - 1))
            last.then_inc(a_done, 1)

            def x_transposes(t, h):
                pe.wait_ge(staged, t + 1)
                if not (isinstance(t, int) and t < 2):
                    pe.wait_ge(xt_lo, t - 1)
                for k in range(KC):
                    last = nc.tensor.transpose(ps[:, PT_BANK + h, k * P:(k + 1) * P], x_stage[:, h, k * P:(k + 1) * P],
                                               ident[:, :])
                last.then_inc(xt_done, 1)

            def v_product(t, h):
                pe.wait_ge(xt_lo, t + 1)
                if not (isinstance(t, int) and t < 2):
                    pe.wait_ge(v_f32, t - 1)
                    pe.wait_ge(r_copied, t - 1)
                for k in range(KC):
                    hi = x_chunk(t, 0, k)
                    nc.tensor.matmul(ps[:, S_BANK + h, :], hi, Ws[:, k, 0, :], start=(k == 0), stop=False)
                    nc.tensor.matmul(ps[:, S_BANK + h, :], hi, Ws[:, k, 1, :], start=False, stop=False)
                    nc.tensor.matmul(ps[:, O_BANK + h, 0:2], hi, wr[:, k, :], start=(k == 0), stop=False)
                    lo = x_chunk(t, 1, k)
                    nc.tensor.matmul(ps[:, S_BANK + h, :], lo, Ws[:, k, 0, :], start=False, stop=(k == KC - 1))
                    last = nc.tensor.matmul(ps[:, O_BANK + h, 0:1], lo, wr[:, k, 0:1], start=False,
                                            stop=(k == KC - 1))
                last.then_inc(v_done, 1)

            x_transposes(0, 0)
            x_transposes(1, 1)
            pe.wait_ge(split_ready, 3)

            def x_and_v(t):
                v_product(t, 0)
                x_transposes(t + 2, 0)
                v_product(t + 1, 1)
                x_transposes(t + 3, 1)

            x_and_v(0)
            with pe.Fori(1, PAIRS - 1) as q:
                x_and_v(q * 2)
            v_product(T - 2, 0)
            v_product(T - 1, 1)

            def u_product(pair):
                for m in range(KC):
                    dst = ps[:, U_BANK + m // 2, (m % 2) * 2 * P:(m % 2 + 1) * 2 * P]
                    for k in range(KC):
                        if isinstance(pair, int):
                            hi, lo = (xT[:, s, k, pair * 2 * P:(pair + 1) * 2 * P] for s in (0, 1))
                        else:
                            hi, lo = (xT[:, s, k, bass.ds(pair * (2 * P), 2 * P)] for s in (0, 1))
                        a_hi, a_lo = A[:, k, 0, m * P:(m + 1) * P], A[:, k, 1, m * P:(m + 1) * P]
                        nc.tensor.matmul(dst, a_hi, hi, start=(k == 0), stop=False)
                        nc.tensor.matmul(dst, a_hi, lo, start=False, stop=False)
                        last = nc.tensor.matmul(dst, a_lo, hi, start=False, stop=(k == KC - 1))
                last.then_inc(u_done, 1)

            def scores(i, par, b):
                n = i * NB + b
                w = widths[b]
                if not (isinstance(n, int) and n < 2):
                    pe.wait_ge(relu_done, n - 1)
                dst = ps[:, S_BANK + (par + b) % 2, 0:w]
                for k in range(KC):
                    u_hi_, u_lo_ = (uT[:, k, s, par * P:(par + 1) * P] for s in (0, 1))
                    x_hi_, x_lo_ = (xT[:, s, k, b * BLOCK:b * BLOCK + w] for s in (0, 1))
                    nc.tensor.matmul(dst, u_hi_, x_hi_, start=(k == 0), stop=False)
                    nc.tensor.matmul(dst, u_hi_, x_lo_, start=False, stop=False)
                    last = nc.tensor.matmul(dst, u_lo_, x_hi_, start=False, stop=(k == KC - 1))
                last.then_inc(scores_done, 1)

            def transposes(i, par, b):
                n = i * NB + b
                pe.wait_ge(exp_done, n + 1)
                if not (isinstance(n, int) and n < 2):
                    pe.wait_ge(pt_lo, n - 1)
                for j in range(widths[b] // P):
                    a = b * BLOCK + j * P
                    last = nc.tensor.transpose(ps[:, PT_BANK + (par + b) % 2, j * P:(j + 1) * P], S[:, par, a:a + P],
                                               ident[:, :])
                last.then_inc(pt_done, 1)

            def attend(i, par, b):
                n = i * NB + b
                pe.wait_ge(pt_lo, n + 1)
                if b == 0 and not (isinstance(i, int) and i < 1):
                    pe.wait_ge(y_ready, i)
                for j in range(widths[b] // P):
                    t = b * JT + j
                    hi, lo = (PT[:, (par + b) % 2, s, j * P:(j + 1) * P] for s in (0, 1))
                    nc.tensor.matmul(ps[:, O_BANK, :], hi, V[:, t, 0, :], start=(t == 0), stop=False)
                    nc.tensor.matmul(ps[:, O_BANK, :], hi, V[:, t, 1, :], start=False, stop=False)
                    last = nc.tensor.matmul(ps[:, O_BANK, :], lo, V[:, t, 0, :], start=False, stop=(t == T - 1))
                last.then_inc(av_done, 1)

            def step(i, par, pair):
                for b in range(NB):
                    if b == NB - 2:
                        transposes(i - 1, 1 - par, 0)
                    scores(i, par, b)
                transposes(i - 1, 1 - par, 1)
                if pair is not None:
                    u_product(pair)
                for b in range(NB):
                    attend(i - 1, 1 - par, b)
                    if b + 2 < NB:
                        transposes(i - 1, 1 - par, b + 2)
                if pair is not None:
                    pe.wait_ge(u_ready, pair + 1)

            pe.wait_ge(v_lo, T)
            pe.wait_ge(r_ready, 1)
            u_product(0)
            pe.wait_ge(u_ready, 1)
            for b in range(NB):
                scores(0, 0, b)
            step(1, 1, 1)
            with pe.Fori(0, PAIRS - 2) as p:
                step(p * 2 + 2, 0, None)
                step(p * 2 + 3, 1, p + 2)
            step(T - 2, 0, None)
            step(T - 1, 1, None)
            transposes(T - 1, 1, 0)
            transposes(T - 1, 1, 1)
            for b in range(NB):
                attend(T - 1, 1, b)
                if b + 2 < NB:
                    transposes(T - 1, 1, b + 2)


_INS = ["x", "adj", "L0_gnn_Wf", "L0_gnn_bf", "L0_gnn_Wg", "L0_gnn_bg", "L0_gnn_W", "L0_gnn_bW"]


def kernel(**inputs):
    import numpy as np
    import concourse.bacc as bacc
    from concourse.bass_utils import run_bass_kernel_spmd

    nc = bacc.Bacc("TRN2", target_bir_lowering=False, num_devices=1)
    arrays, args = {}, []
    for name in _INS:
        a = np.ascontiguousarray(inputs[name])
        arrays[f"in_{name}"] = a
        args.append(nc.dram_tensor(f"in_{name}", a.shape, mybir.dt.from_np(a.dtype), kind="ExternalInput").ap())
    out = nc.dram_tensor("out", inputs["x"].shape, F32, kind="ExternalOutput").ap()
    gnn_kernel(nc, *args, out)
    r = run_bass_kernel_spmd(nc, [arrays], core_ids=[0])
    return r.results[0]["out"]
```

```python
from contextlib import ExitStack

import concourse.bass as bass
from concourse import mybir

ALU = mybir.AluOpType
ACT = mybir.ActivationFunctionType
AX = mybir.AxisListType
F32 = mybir.dt.float32
F16 = mybir.dt.float16
BF16 = mybir.dt.bfloat16
I32 = mybir.dt.int32
RED_MAX = bass.bass_isa.ReduceOp.max

P = 128
BW = 2 * P
EPS = 1e-5
TOP = 14
PSCALE = float(2 ** TOP)
MASKED = -float(2.0 ** 126)
PAD_BIAS = -1e30
LEAST_MAX = float(2.0 ** -30)
EXPONENT_BITS = 0x7F800000
SCALE_BITS = float((TOP + 2 * 127) << 23)


def gnn_kernel(nc, x_rows, xT_blocks, adjT_blocks, WfT, bf_cols, WgT, bg_cols, W, bW, out):
    NP, D = x_rows.shape
    NBLK = xT_blocks.shape[0]
    KC = D // P
    T = NP // P
    CH = T // 2
    assert NBLK == NP // BW == CH and NBLK % 2 == 1 and KC == 4
    EARLY = 8
    XPIECES = [(0, 3), (3, 6), (6, 9), (9, 11), (11, NBLK)]

    with ExitStack() as ctx:
        def sb(name, shape, dt):
            return ctx.enter_context(nc.sbuf_tensor(name, shape, dt))

        def sem(name):
            return ctx.enter_context(nc.semaphore(name))

        w_all = sb("w_all", [P, KC, 2, NP], F16)
        V = sb("V", [P, T, 2, D], F16)
        x_all = V[:, :, :, :].rearrange("p t s d -> p (t s d)").bitcast(F32).rearrange("p (b n) -> p b n", b=NBLK)
        ident = sb("ident", [P, P], F32)
        ones = sb("ones", [P, P], F32)
        b_all = sb("b_all", [P, T], F32)
        S = sb("S", [P, 2, CH, 2 * BW], F32)
        att = S[:, :, :, :].rearrange("p b c n -> p (b c n)").bitcast(F16).rearrange(
            "p (b c s n) -> p b c s n", b=2, c=CH, s=2)
        adj_t = sb("adj_t", [P, CH, 2 * BW], I32)
        penalty = sb("penalty", [P, 2, 2 * BW], BF16)
        E = sb("E", [P, 3, 2 * BW], F32)
        x32 = sb("x32", [P, KC, BW], F32)
        xb = sb("xb", [P, 2, KC, BW], F16)
        top = sb("top", [P, 2 * BW], F32)
        top2 = sb("top2", [P, BW], F32)
        diag = sb("diag", [P, 2, P], F32)
        total = sb("total", [P, 2 * BW], F32)
        total2 = sb("total2", [P, BW], F32)
        y = sb("y", [P, 2, D], F32)
        flat0 = S[:, 0, :, :].rearrange("p c n -> p (c n)")
        flat1 = S[:, 1, :, :].rearrange("p c n -> p (c n)")
        flat_adj = adj_t[:, :, :].rearrange("p c n -> p (c n)").bitcast(F32)
        KD = KC * D
        WfT_n = flat_adj[:, 0:KD].rearrange("p (c d) -> p c d", c=KC)
        WgT_n = flat_adj[:, KD:2 * KD].rearrange("p (c d) -> p c d", c=KC)
        z = flat_adj[:, 2 * KD:2 * KD + 2 * D].rearrange("p (s d) -> p s d", s=2)
        W_n = flat0[:, 0:KD].rearrange("p (c d) -> p c d", c=KC)
        Ws = flat0[:, KD:2 * KD].bitcast(F16).rearrange("p (c s d) -> p c s d", c=KC, s=2)
        B = flat0[:, 2 * KD:3 * KD].bitcast(F16).rearrange("p (c s d) -> p c s d", c=KC, s=2)
        xp = flat1[:, 0:KC * BW * 2].bitcast(F16).rearrange("p (b s c n) -> p b s c n", b=2, s=2, c=KC)
        w32 = flat1[:, 2048:3072].rearrange("p (c n) -> p c n", c=KC)
        v32 = flat1[:, 3072:4096].rearrange("p (b d) -> p b d", b=2)
        bWs = flat1[:, 4096:4608]
        bf_c = sb("bf_c", [P, KC], F32)
        bg_c = sb("bg_c", [P, KC], F32)
        bb_c = sb("bb_c", [P, KC], F32)
        bb_1 = sb("bb_1", [P, 1], F32)
        c_col = sb("c_col", [P, KC], F32)
        cs_col = sb("cs_col", [P, KC], F32)
        vb32 = sb("vb32", [P, KC], F32)
        vb = sb("vb", [P, KC, 2], F16)
        b_part = sb("b_part", [P, T, 2], F32)
        xmax = sb("xmax", [P, 8], F32)
        stats = sb("stats", [P, 8], F32)
        stats_all = sb("stats_all", [P, 8], F32)
        sc = sb("sc", [P, 40], F32)
        pad_bias = sb("pad_bias", [P, 1], F32)
        top_col = sb("top_col", [P, 2], F32)
        fin = sb("fin", [P, 2, 8], F32)
        bn6 = sb("bn6", [P, 2, 6], F32)
        bn2 = sb("bn2", [P, 2, 2], F32)
        neg_half = sb("neg_half", [P, 1], F32)
        carrier = sb("carrier", [P, 2], F32)

        ps = ctx.enter_context(nc.psum_tensor("ps", [P, 8, 512], F32))
        S_BANK, O_BANK, TOP_BANK, MAX_BANK, SUM_BANK = 0, 3, 5, 6, 7
        SMALL_BANK, PROD_BANK, W_BANK, V_BANK, B_BANK = 0, 4, 0, 4, 6

        wT_in = sem("wT_in")
        w_in = sem("w_in")
        biases_in = sem("biases_in")
        bW_in = sem("bW_in")
        x_in = [sem(f"x_in{n}") for n in range(len(XPIECES))]
        ident_zeroed = sem("ident_zeroed")
        ident_ready = sem("ident_ready")
        ones_ready = sem("ones_ready")
        half_ready = sem("half_ready")
        z_ready = sem("z_ready")
        product_done = sem("product_done")
        small_done = sem("small_done")
        prep = sem("prep")
        stats_ready = sem("stats_ready")
        stats_summed = sem("stats_summed")
        scales_ready = sem("scales_ready")
        split_hi = sem("split_hi")
        split_ready = sem("split_ready")
        xp_hi = sem("xp_hi")
        xp_lo = sem("xp_lo")
        w_done = sem("w_done")
        w_f32 = sem("w_f32")
        w_hi = sem("w_hi")
        w_lo = sem("w_lo")
        v_done = sem("v_done")
        v_f32 = sem("v_f32")
        v_hi = sem("v_hi")
        v_lo = sem("v_lo")
        b_copied = sem("b_copied")
        b_ready = sem("b_ready")
        adj_in = sem("adj_in")
        x32_in = sem("x32_in")
        xb_hi = sem("xb_hi")
        xb_lo = sem("xb_lo")
        y_in = sem("y_in")
        scores_done = sem("scores_done")
        relu_done = sem("relu_done")
        penalty_ready = sem("penalty_ready")
        masked = sem("masked")
        topped = sem("topped")
        top2_ready = sem("top2_ready")
        top_turned = sem("top_turned")
        top_col_ready = sem("top_col_ready")
        diag_ready = sem("diag_ready")
        max_done = sem("max_done")
        lowered = sem("lowered")
        exp_done = sem("exp_done")
        att_hi = sem("att_hi")
        att_lo = sem("att_lo")
        summed = sem("summed")
        total2_ready = sem("total2_ready")
        sum_turned = sem("sum_turned")
        av_done = sem("av_done")
        norm = sem("norm")
        y_ready = sem("y_ready")
        rstd_ready = sem("rstd_ready")
        out_ready = sem("out_ready")
        stored = sem("stored")

        (mB, mW, mX, mU, mV, sB, sW, sX, sU, sV, t0, t1, unit_BX, unit_WX, iBX, iWX, ratio_w, ratio_v,
         iB, ratio_b, UX, score_unit, beta, iV, out_unit) = range(25)

        def col(k, n=1):
            return sc[:, k:k + n]

        def at(ap, k):
            return ap[:, k] if isinstance(k, int) else ap[:, bass.ds(k, 1)].squeeze(1)

        def wait_for(eng, signal, value):
            if not (isinstance(value, int) and value <= 0):
                eng.wait_ge(signal, value)

        def wait_apart(dve, signal, value, word):
            dve.wait_ge(signal, value)
            nc.vector.memset(carrier[:, word:word + 1], 0.0)

        def w_block(b, half):
            cols = slice(b * BW, (b + 1) * BW) if isinstance(b, int) else bass.ds(b * BW, BW)
            return w_all[:, :, half, cols]

        def since(c):
            return 3 if c >= 3 else CH - max(k for k in range(CH) if k % 3 == c % 3) + c

        block = ctx.enter_context(nc.Block())

        @block.sync
        def _(sp):
            sp.dma_start(WgT_n, WgT).then_inc(wT_in, 16)
            sp.dma_start(WfT_n, WfT).then_inc(wT_in, 16)
            for n, (a, b) in enumerate(XPIECES):
                sp.dma_start(x_all[:, a:b, :], xT_blocks[a:b].rearrange("b p n -> p b n")).then_inc(x_in[n], 16)

            def load_adj(s):
                src = adjT_blocks[s] if isinstance(s, int) else adjT_blocks[bass.ds(s, 1)].squeeze(0)
                sp.dma_start(adj_t[:, :, :].rearrange("p c n -> p (c n)"), src).then_inc(adj_in, 16)

            def load_x32(s):
                src = xT_blocks[s] if isinstance(s, int) else xT_blocks[bass.ds(s, 1)].squeeze(0)
                sp.dma_start(x32[:, :, :].rearrange("p c n -> p (c n)"), src).then_inc(x32_in, 16)

            def rows(ap, s):
                r = ap[s * BW:(s + 1) * BW] if isinstance(s, int) else ap[bass.ds(s * BW, BW)]
                return r.rearrange("(h p) d -> p h d", p=P)

            load_x32(0)
            sp.dma_start(y[:, :, :], rows(x_rows, 0)).then_inc(y_in, 16)
            sp.wait_ge(product_done, 1)
            sp.wait_ge(small_done, 1)
            load_adj(0)

            def step(s, more):
                if more:
                    wait_for(sp, xb_lo, s + 1)
                    load_x32(s + 1)
                    sp.wait_ge(penalty_ready, (s + 1) * CH)
                    load_adj(s + 1)
                if not (isinstance(s, int) and s == 0):
                    sp.wait_ge(out_ready, s * 2)
                    sp.dma_start(rows(out, s - 1), y[:, :, :]).then_inc(stored, 16)
                    sp.wait_ge(stored, s * 16)
                    sp.dma_start(y[:, :, :], rows(x_rows, s)).then_inc(y_in, 16)

            step(0, True)
            step(1, True)
            with sp.Fori(0, NBLK // 2 - 1) as q:
                step(q * 2 + 2, True)
                step(q * 2 + 3, True)
            step(NBLK - 1, False)
            sp.wait_ge(out_ready, 2 * NBLK)
            sp.dma_start(rows(out, NBLK - 1), y[:, :, :]).then_inc(stored, 16)
            sp.wait_ge(stored, 16 * NBLK)

        @block.gpsimd
        def _(pool):
            nc.gpsimd.memset(ident[:, :], 0.0).then_inc(ident_zeroed, 1)
            pool.wait_ge(ident_zeroed, 1)
            nc.gpsimd.affine_select(out=ident[:, :], in_=ident[:, :], compare_op=ALU.not_equal, fill=1.0, base=0,
                                    pattern=[[-1, P]], channel_multiplier=1).then_inc(ident_ready, 1)
            nc.gpsimd.memset(neg_half[:, :], -0.5).then_inc(half_ready, 1)
            pool.wait_ge(half_ready, 1)
            pool.wait_ge(ones_ready, 1)
            pool.wait_ge(stats_ready, 1)
            nc.gpsimd.partition_all_reduce(stats_all[:, 0:4], stats[:, 0:4], P, RED_MAX).then_inc(stats_summed, 1)
            pool.wait_ge(stats_ready, 2)
            nc.gpsimd.partition_all_reduce(stats_all[:, 5:6], stats[:, 5:6], P, RED_MAX).then_inc(stats_summed, 1)

            def sums(s, chunks):
                for c in chunks:
                    n = s * CH + c
                    pool.wait_ge(exp_done, n + 1)
                    if c == 0:
                        wait_for(pool, total2_ready, s)
                        nc.gpsimd.tensor_tensor(total[:, :].rearrange("p (a n) -> p a n", n=P),
                                                E[:, 0, :].rearrange("p (a n) -> p a n", n=P),
                                                ones[:, :].unsqueeze(1).to_broadcast([P, 2 * BW // P, P]),
                                                ALU.mult).then_inc(summed, 1)
                    else:
                        pool.wait_ge(summed, n)
                        nc.gpsimd.tensor_tensor(total[:, :], total[:, :], E[:, c % 3, :], ALU.add).then_inc(summed, 1)
                if chunks[-1] == CH - 1:
                    pool.wait_ge(summed, (s + 1) * CH)
                    wait_for(pool, sum_turned, s)
                    nc.gpsimd.tensor_tensor(total2[:, :], total[:, 0:BW], total[:, BW:2 * BW],
                                            ALU.add).then_inc(total2_ready, 1)

            def rstd(s, h):
                pool.wait_ge(norm, (s * 2 + h + 1) * 6)
                nc.gpsimd.tensor_tensor(fin[:, h, 5:6], fin[:, h, 4:5], neg_half[:, :], ALU.pow).then_inc(rstd_ready, 1)

            def step(s, early):
                if early[0] > 0:
                    sums(s - 1, range(early[0], CH))
                rstd_first = early[1] // 2
                if rstd_first:
                    sums(s, range(0, rstd_first))
                rstd(s - 1, 0)
                if early[1] > rstd_first:
                    sums(s, range(rstd_first, early[1]))
                rstd(s - 1, 1)

            sums(0, range(0, CH))
            step(1, (0, EARLY))
            with pool.Fori(0, NBLK // 2 - 1) as q:
                step(q * 2 + 2, (EARLY, EARLY))
                step(q * 2 + 3, (EARLY, EARLY))
            step(NBLK - 1, (EARLY, CH))
            rstd(NBLK - 1, 0)
            rstd(NBLK - 1, 1)

        @block.scalar
        def _(act):
            act.dma_start(bf_c[:, :], bf_cols).then_inc(biases_in, 16)
            act.dma_start(bg_c[:, :], bg_cols).then_inc(biases_in, 16)
            act.dma_start(W_n, W.rearrange("(c p) d -> p c d", p=P)).then_inc(w_in, 16)
            act.dma_start(bWs, bW.rearrange("(a d) -> a d", a=1).to_broadcast([P, D])).then_inc(bW_in, 16)
            act.wait_ge(scales_ready, 1)
            for c in range(KC):
                nc.scalar.activation(B[:, c, 0, :], ps[:, PROD_BANK + c, :], ACT.Copy, scale=col(sB)).then_inc(split_hi, 1)
            act.wait_ge(w_in, 16)
            nc.scalar.activation(Ws[:, :, 0, :], W_n, ACT.Copy, scale=col(sW)).then_inc(split_hi, 1)

            def xp_split(b, par):
                wait_for(act, v_done, (b - 1) * 2)
                nc.scalar.activation(xp[:, par, 0, :, :].rearrange("p c n -> p (c n)"), at(x_all, b), ACT.Copy,
                                     scale=col(sX)).then_inc(xp_hi, 1)

            def w_split(b, par):
                act.wait_ge(w_done, b + 1)
                wait_for(act, w_lo, b)
                for m in range(KC):
                    last = nc.scalar.activation(w32[:, m, :], ps[:, W_BANK + 2 * par + m // 2, m % 2 * BW:(m % 2 + 1) * BW],
                                                ACT.Identity, bias=cs_col[:, m:m + 1], scale=col(ratio_w))
                last.then_inc(w_f32, 1)
                act.wait_ge(w_f32, b + 1)
                nc.scalar.copy(w_block(b, 0), w32).then_inc(w_hi, 1)

            def v_split(t, h):
                act.wait_ge(v_f32, t + 1)
                nc.scalar.copy(at(V, t)[:, 0, :], v32[:, h, :]).then_inc(v_hi, 1)

            act.wait_ge(scales_ready, 2)
            xp_split(0, 0)
            act.wait_ge(scales_ready, 3)

            def prepare(b, par, more=True):
                if more:
                    xp_split(b + 1, 1 - par)
                w_split(b, par)
                v_split(b * 2, 0)
                v_split(b * 2 + 1, 1)

            prepare(0, 0)
            with act.Fori(0, NBLK // 2 - 1) as q:
                prepare(q * 2 + 1, 1)
                prepare(q * 2 + 2, 0)
            prepare(NBLK - 2, 1)
            prepare(NBLK - 1, 0, False)

            def x_split(s):
                act.wait_ge(x32_in, s * 16 + 16)
                wait_for(act, scores_done, s * CH)
                nc.scalar.activation(xb[:, 0, :, :], x32[:, :, :], ACT.Copy, scale=col(sX)).then_inc(xb_hi, 1)

            def relu(s, par, c):
                act.wait_ge(scores_done, s * CH + c + 1)
                for h in range(2):
                    last = nc.scalar.activation(S[:, par, c, h * BW:(h + 1) * BW],
                                                ps[:, S_BANK + c % 3, h * BW:(h + 1) * BW], ACT.Relu,
                                                bias=b_all[:, 2 * c + h:2 * c + h + 1])
                last.then_inc(relu_done, 1)

            def soften(s, par, c):
                n = s * CH + c
                act.wait_ge(lowered, n + 1)
                wait_for(act, att_lo, n + 1 - since(c))
                wait_for(act, summed, n + 1 - since(c))
                if c < CH - 1:
                    last = nc.scalar.activation(E[:, c % 3, :], S[:, par, c, :], ACT.Exp, scale=col(score_unit))
                else:
                    nc.scalar.activation(E[:, c % 3, 0:BW], S[:, par, c, 0:BW], ACT.Exp, scale=col(score_unit))
                    last = nc.scalar.activation(E[:, c % 3, BW:2 * BW], S[:, par, c, BW:2 * BW], ACT.Exp,
                                                bias=pad_bias[:, :], scale=col(score_unit))
                last.then_inc(exp_done, 1)
                act.wait_ge(exp_done, n + 1)
                nc.scalar.activation(att[:, par, c, 0, :], E[:, c % 3, :], ACT.Copy, scale=PSCALE).then_inc(att_hi, 1)

            def step(s, par, early):
                left = list(range(early[0], CH))
                for c in range(CH):
                    relu(s, par, c)
                    if early[0] == 0:
                        if c >= 3 and left:
                            soften(s - 1, 1 - par, left.pop(0))
                    elif c % 2 == 1 and left:
                        soften(s - 1, 1 - par, left.pop(0))
                while left:
                    soften(s - 1, 1 - par, left.pop(0))
                if early[1] < CH:
                    x_split(s + 1)
                for c in range(early[1]):
                    soften(s, par, c)

            act.wait_ge(b_ready, 1)
            x_split(0)
            for c in range(CH):
                relu(0, 0, c)
            x_split(1)
            step(1, 1, (0, EARLY))
            with act.Fori(0, NBLK // 2 - 1) as q:
                step(q * 2 + 2, 0, (EARLY, EARLY))
                step(q * 2 + 3, 1, (EARLY, EARLY))
            step(NBLK - 1, 0, (EARLY, CH))

        @block.vector
        def _(dve):
            done = [0]

            def link(ins):
                done[0] += 1
                ins.then_inc(prep, 1)
                dve.wait_ge(prep, done[0])

            def amax(dst, src):
                return nc.vector.tensor_reduce(dst, src, AX.X if len(src.shape) == 2 else AX.XY, ALU.max,
                                               apply_absolute_value=True)

            nc.vector.memset(ones[:, :], 1.0).then_inc(ones_ready, 1)
            nc.vector.memset(stats[:, :], 0.0)
            dve.wait_ge(biases_in, 32)
            nc.vector.tensor_tensor(bb_c[:, :], bf_c[:, :], bg_c[:, :], ALU.mult)
            dve.wait_ge(wT_in, 32)
            for c in range(KC):
                for s, (w, b) in enumerate(((WfT_n, bg_c), (WgT_n, bf_c))):
                    if c == 0:
                        last = nc.vector.tensor_scalar(z[:, s, :], w[:, 0, :], b[:, 0:1], None, ALU.mult)
                    else:
                        last = nc.vector.scalar_tensor_tensor(z[:, s, :], w[:, c, :], b[:, c:c + 1], z[:, s, :],
                                                              ALU.mult, ALU.add)
                link(last)
            nc.vector.tensor_reduce(bb_1[:, :], bb_c[:, :], AX.X, ALU.add).then_inc(z_ready, 1)
            def x_max(n):
                a, b = XPIECES[n]
                dve.wait_ge(x_in[n], 16)
                return amax(xmax[:, n:n + 1], x_all[:, a:b, :])

            dve.wait_ge(w_in, 16)
            amax(stats[:, 1:2], W_n)
            dve.wait_ge(bW_in, 16)
            amax(stats[:, 2:3], bWs)
            x_max(0)
            x_max(1)
            dve.wait_ge(small_done, 1)
            dve.wait_ge(product_done, 1)
            amax(sc[:, 30:31], ps[:, PROD_BANK:PROD_BANK + KC, :])
            amax(stats[:, 3:4], ps[:, SMALL_BANK, 0:KC])
            amax(sc[:, 31:32], ps[:, SMALL_BANK, KC:2 * KC])
            nc.vector.tensor_copy(c_col[:, :], ps[:, SMALL_BANK, 0:KC])
            nc.vector.tensor_copy(vb32[:, :], ps[:, SMALL_BANK, KC:2 * KC])
            link(nc.vector.tensor_copy(col(beta), ps[:, SMALL_BANK, 2 * KC:2 * KC + 1]))
            nc.vector.tensor_tensor(stats[:, 0:1], sc[:, 30:31], sc[:, 31:32], ALU.max).then_inc(stats_ready, 1)
            x_max(2)

            def scale_of(dst, maximum, n):
                link(nc.vector.tensor_scalar(col(t0, n), maximum, LEAST_MAX, None, ALU.max))
                link(nc.vector.tensor_scalar(col(t0, n).bitcast(I32), col(t0, n).bitcast(I32), EXPONENT_BITS, None,
                                             ALU.bitwise_and))
                return nc.vector.tensor_scalar(dst.bitcast(I32), col(t0, n).bitcast(I32), -1.0, SCALE_BITS,
                                               ALU.mult, ALU.add)

            dve.wait_ge(stats_summed, 1)
            link(nc.vector.tensor_scalar(col(mB, 2), stats_all[:, 0:2], LEAST_MAX, None, ALU.max))
            scale_of(col(sB, 2), col(mB, 2), 2).then_inc(scales_ready, 1)
            for c in range(KC):
                dve.wait_ge(split_hi, c + 1)
                last = nc.vector.scalar_tensor_tensor(B[:, c, 1, :], ps[:, PROD_BANK + c, :], col(sB), B[:, c, 0, :],
                                                      ALU.mult, ALU.subtract)
            last.then_inc(split_ready, 1)
            link(nc.vector.tensor_scalar(vb32[:, :], vb32[:, :], col(sB), None, ALU.mult))
            link(nc.vector.tensor_copy(vb[:, :, 0], vb32[:, :]))
            nc.vector.tensor_tensor(vb[:, :, 1], vb32[:, :], vb[:, :, 0], ALU.subtract).then_inc(split_ready, 1)
            for n in range(3, len(XPIECES)):
                last = x_max(n)
            link(last)
            nc.vector.tensor_reduce(stats[:, 5:6], xmax[:, 0:len(XPIECES)], AX.X, ALU.max).then_inc(stats_ready, 1)
            dve.wait_ge(split_hi, KC + 1)
            nc.vector.scalar_tensor_tensor(Ws[:, :, 1, :], W_n, col(sW), Ws[:, :, 0, :], ALU.mult,
                                           ALU.subtract).then_inc(split_ready, 1)
            dve.wait_ge(stats_summed, 2)
            link(nc.vector.tensor_scalar(col(mX), stats_all[:, 5:6], LEAST_MAX, None, ALU.max))
            last = scale_of(col(sX), col(mX), 1)
            last.then_inc(scales_ready, 1)
            dve.wait_ge(scales_ready, 2)

            def xp_lo_part(b, par):
                dve.wait_ge(xp_hi, b + 1)
                nc.vector.scalar_tensor_tensor(xp[:, par, 1, :, :].rearrange("p c n -> p (c n)"), at(x_all, b), col(sX),
                                               xp[:, par, 0, :, :].rearrange("p c n -> p (c n)"), ALU.mult,
                                               ALU.subtract).then_inc(xp_lo, 1)

            xp_lo_part(0, 0)
            link(nc.vector.tensor_scalar(col(mU, 2), col(mB, 2), col(mX), float(D), ALU.mult, ALU.mult))
            nc.vector.tensor_tensor(col(mV), col(mV), stats_all[:, 2:3], ALU.add)
            link(nc.vector.tensor_tensor(col(mU), col(mU), stats_all[:, 3:4], ALU.add))
            link(scale_of(col(sU, 2), col(mU, 2), 2))
            link(nc.vector.tensor_scalar(col(unit_BX, 2), col(sB, 2), col(sX), None, ALU.mult))
            link(nc.vector.reciprocal(col(iBX, 2), col(unit_BX, 2)))
            nc.vector.tensor_scalar(cs_col[:, :], c_col[:, :], col(sU), None, ALU.mult)
            nc.vector.tensor_scalar(bWs, bWs, col(sV), None, ALU.mult)
            link(nc.vector.tensor_tensor(col(ratio_w, 2), col(iBX, 2), col(sU, 2), ALU.mult))
            nc.vector.tensor_tensor(col(UX), col(sU), col(sX), ALU.mult).then_inc(scales_ready, 1)
            dve.wait_ge(scales_ready, 3)
            nc.vector.reciprocal(col(score_unit), col(UX))
            link(nc.vector.reciprocal(col(iB), col(sB)))
            nc.vector.tensor_tensor(col(ratio_b), col(sU), col(iB), ALU.mult)
            nc.vector.tensor_tensor(col(beta), col(beta), col(UX), ALU.mult)
            link(nc.vector.reciprocal(col(iV), col(sV)))
            nc.vector.tensor_scalar(col(out_unit), col(iV), 1.0 / PSCALE, None, ALU.mult)
            dve.wait_ge(ident_ready, 1)
            link(nc.vector.tensor_scalar(pad_bias[:, :], ident[:, P - 1:P], PAD_BIAS, None, ALU.mult))

            def v_from(t, h):
                dve.wait_ge(v_done, t + 1)
                wait_for(dve, v_hi, t - 1)
                nc.vector.scalar_tensor_tensor(v32[:, h, :], ps[:, V_BANK + h, :], col(ratio_v), bWs, ALU.mult,
                                               ALU.add).then_inc(v_f32, 1)
                nc.vector.tensor_copy(at(b_part, t), ps[:, B_BANK + h, 0:2]).then_inc(b_copied, 1)

            def v_lo_part(t, h):
                dve.wait_ge(v_hi, t + 1)
                nc.vector.tensor_tensor(at(V, t)[:, 1, :], v32[:, h, :], at(V, t)[:, 0, :], ALU.subtract).then_inc(v_lo, 1)

            def prepare(b, par, more=True):
                if more:
                    xp_lo_part(b + 1, 1 - par)
                dve.wait_ge(w_hi, b + 1)
                nc.vector.tensor_tensor(w_block(b, 1), w32, w_block(b, 0), ALU.subtract).then_inc(w_lo, 1)
                v_from(b * 2, 0)
                v_lo_part(b * 2, 0)
                v_from(b * 2 + 1, 1)
                v_lo_part(b * 2 + 1, 1)

            prepare(0, 0)
            with dve.Fori(0, NBLK // 2 - 1) as q:
                prepare(q * 2 + 1, 1)
                prepare(q * 2 + 2, 0)
            prepare(NBLK - 2, 1)
            prepare(NBLK - 1, 0, False)
            dve.wait_ge(b_copied, T)
            link(nc.vector.tensor_tensor(b_all[:, :], b_part[:, :, 0], b_part[:, :, 1], ALU.add))
            nc.vector.tensor_scalar(b_all[:, :], b_all[:, :], col(ratio_b), col(beta), ALU.mult,
                                    ALU.add).then_inc(b_ready, 1)

            def x_split(s):
                dve.wait_ge(xb_hi, s + 1)
                nc.vector.scalar_tensor_tensor(xb[:, 1, :, :].rearrange("p c n -> p (c n)"),
                                               x32[:, :, :].rearrange("p c n -> p (c n)"), col(sX),
                                               xb[:, 0, :, :].rearrange("p c n -> p (c n)"), ALU.mult,
                                               ALU.subtract).then_inc(xb_lo, 1)

            def mask(s, par, c):
                n = s * CH + c
                if c == 0:
                    dve.wait_ge(adj_in, s * 16 + 16)
                nc.vector.tensor_scalar(penalty[:, (par + c) % 2, :], adj_t[:, c, :], 0.0, MASKED, ALU.is_le,
                                        ALU.mult).then_inc(penalty_ready, 1)
                dve.wait_ge(relu_done, n + 1)
                dve.wait_ge(penalty_ready, n + 1)
                nc.vector.tensor_tensor(S[:, par, c, :], S[:, par, c, :], penalty[:, (par + c) % 2, :],
                                        ALU.add).then_inc(masked, 1)
                dve.wait_ge(masked, n + 1)
                if c == 0:
                    nc.vector.tensor_copy(top[:, :], S[:, par, c, :]).then_inc(topped, 1)
                else:
                    dve.wait_ge(topped, n)
                    nc.vector.tensor_tensor(top[:, :], top[:, :], S[:, par, c, :], ALU.max).then_inc(topped, 1)

            def finish_max(s):
                dve.wait_ge(topped, (s + 1) * CH)
                nc.vector.tensor_tensor(top2[:, :], top[:, 0:BW], top[:, BW:2 * BW], ALU.max).then_inc(top2_ready, 1)
                dve.wait_ge(top_turned, s + 1)
                nc.vector.tensor_reduce(top_col[:, :], ps[:, TOP_BANK, 0:BW].rearrange("p (h n) -> p h n", h=2), AX.X,
                                        ALU.max).then_inc(top_col_ready, 1)
                dve.wait_ge(top_col_ready, s + 1)
                for h in range(2):
                    last = nc.vector.tensor_scalar(diag[:, h, :], ident[:, :], top_col[:, h:h + 1], None, ALU.mult)
                last.then_inc(diag_ready, 1)

            def lower(s, par, c):
                if c == 0:
                    dve.wait_ge(max_done, s + 1)
                chunk = S[:, par, c, :].rearrange("p (h n) -> p h n", h=2)
                nc.vector.tensor_tensor(chunk, chunk, ps[:, MAX_BANK, 0:BW].unsqueeze(1).to_broadcast([P, 2, BW]),
                                        ALU.subtract).then_inc(lowered, 1)

            def att_lo_part(s, par, c):
                dve.wait_ge(att_hi, s * CH + c + 1)
                nc.vector.scalar_tensor_tensor(att[:, par, c, 1, :], E[:, c % 3, :], PSCALE, att[:, par, c, 0, :],
                                               ALU.mult, ALU.subtract).then_inc(att_lo, 1)

            def finish(s, h):
                t = s * 2 + h
                k = t * 6
                f = fin[:, h, :]
                if h == 0:
                    dve.wait_ge(sum_turned, s + 1)
                nc.vector.tensor_reduce(f[:, 0:1], ps[:, SUM_BANK, h * P:(h + 1) * P], AX.X, ALU.add).then_inc(norm, 1)
                dve.wait_ge(norm, k + 1)
                nc.vector.reciprocal(f[:, 1:2], f[:, 0:1]).then_inc(norm, 1)
                dve.wait_ge(norm, k + 2)
                nc.vector.tensor_scalar(f[:, 2:3], f[:, 1:2], col(out_unit), None, ALU.mult).then_inc(norm, 1)
                dve.wait_ge(norm, k + 3)
                dve.wait_ge(av_done, t + 1)
                dve.wait_ge(y_in, s * 16 + 16)
                nc.vector.scalar_tensor_tensor(y[:, h, :], ps[:, O_BANK + h, :], f[:, 2:3], y[:, h, :], ALU.mult,
                                               ALU.add).then_inc(y_ready, 1)
                dve.wait_ge(y_ready, t + 1)
                nc.vector.bn_stats(bn6[:, h, :], y[:, h, :]).then_inc(norm, 1)
                wait_apart(dve, norm, k + 4, h)
                nc.vector.bn_aggr(bn2[:, h, :], bn6[:, h, :]).then_inc(norm, 1)
                dve.wait_ge(norm, k + 5)
                nc.vector.tensor_scalar(f[:, 4:5], bn2[:, h, 1:2], EPS, None, ALU.add).then_inc(norm, 1)
                dve.wait_ge(rstd_ready, t + 1)
                nc.vector.tensor_scalar(y[:, h, :], y[:, h, :], bn2[:, h, 0:1], f[:, 5:6], ALU.subtract,
                                        ALU.mult).then_inc(out_ready, 1)

            def soften(s, par, chunks):
                chunks = list(chunks)
                if not chunks:
                    return
                lower(s, par, chunks[0])
                for c in chunks[1:]:
                    lower(s, par, c)
                    att_lo_part(s, par, c - 1)
                att_lo_part(s, par, chunks[-1])

            def step(s, par, early):
                left = list(range(early[0], CH))
                if early[0] == 0:
                    finish_max(s - 1)
                ahead = None
                for c in range(CH):
                    mask(s, par, c)
                    if left and (c >= 3 if early[0] == 0 else c % 2 == 0):
                        k = left.pop(0)
                        lower(s - 1, 1 - par, k)
                        if ahead is not None:
                            att_lo_part(s - 1, 1 - par, ahead)
                        ahead = k
                if left:
                    for k in left:
                        lower(s - 1, 1 - par, k)
                        att_lo_part(s - 1, 1 - par, ahead)
                        ahead = k
                att_lo_part(s - 1, 1 - par, ahead)
                if early[1] < CH:
                    x_split(s + 1)
                finish_max(s)
                soften(s, par, range(0, early[1] // 2))
                finish(s - 1, 0)
                soften(s, par, range(early[1] // 2, early[1]))
                finish(s - 1, 1)

            x_split(0)
            for c in range(CH):
                mask(0, 0, c)
            x_split(1)
            step(1, 1, (0, EARLY))
            with dve.Fori(0, NBLK // 2 - 1) as q:
                step(q * 2 + 2, 0, (EARLY, EARLY))
                step(q * 2 + 3, 1, (EARLY, EARLY))
            step(NBLK - 1, 0, (EARLY, CH))
            finish(NBLK - 1, 0)
            finish(NBLK - 1, 1)

        @block.tensor
        def _(pe):
            pe.wait_ge(wT_in, 32)
            for m in range(KC):
                for k in range(KC):
                    last = nc.tensor.matmul(ps[:, PROD_BANK + m, :], WgT_n[:, k, m * P:(m + 1) * P], WfT_n[:, k, :],
                                            start=(k == 0), stop=(k == KC - 1))
            last.then_inc(product_done, 1)
            pe.wait_ge(ones_ready, 1)
            pe.wait_ge(z_ready, 1)
            for s in range(2):
                for m in range(KC):
                    nc.tensor.matmul(ps[:, SMALL_BANK, s * KC + m:s * KC + m + 1], z[:, s, m * P:(m + 1) * P],
                                     ones[:, 0:1], start=True, stop=True)
            nc.tensor.matmul(ps[:, SMALL_BANK, 2 * KC:2 * KC + 1], ones[:, :], bb_1[:, :], start=True,
                             stop=True).then_inc(small_done, 1)

            def prepare(b, par):
                pe.wait_ge(xp_lo, b + 1)
                wait_for(pe, w_f32, b - 1)
                for m in range(KC):
                    dst = ps[:, W_BANK + 2 * par + m // 2, m % 2 * BW:(m % 2 + 1) * BW]
                    for k in range(KC):
                        hi, lo = (B[:, k, s, m * P:(m + 1) * P] for s in range(2))
                        nc.tensor.matmul(dst, hi, xp[:, par, 0, k, :], start=(k == 0), stop=False)
                        nc.tensor.matmul(dst, hi, xp[:, par, 1, k, :], start=False, stop=False)
                        last = nc.tensor.matmul(dst, lo, xp[:, par, 0, k, :], start=False, stop=(k == KC - 1))
                last.then_inc(w_done, 1)
                for h in range(2):
                    t = b * 2 + h
                    wait_for(pe, v_f32, t - 1)
                    wait_for(pe, b_copied, t - 1)
                    for k in range(KC):
                        hi, lo = (xp[:, par, s, k, h * P:(h + 1) * P] for s in range(2))
                        nc.tensor.matmul(ps[:, V_BANK + h, :], hi, Ws[:, k, 0, :], start=(k == 0), stop=False)
                        nc.tensor.matmul(ps[:, V_BANK + h, :], hi, Ws[:, k, 1, :], start=False, stop=False)
                        nc.tensor.matmul(ps[:, B_BANK + h, 0:2], hi, vb[:, k, :], start=(k == 0), stop=False)
                        nc.tensor.matmul(ps[:, V_BANK + h, :], lo, Ws[:, k, 0, :], start=False, stop=(k == KC - 1))
                        last = nc.tensor.matmul(ps[:, B_BANK + h, 0:1], lo, vb[:, k, 0:1], start=False,
                                                stop=(k == KC - 1))
                    last.then_inc(v_done, 1)

            pe.wait_ge(split_ready, 3)
            prepare(0, 0)
            with pe.Fori(0, NBLK // 2 - 1) as q:
                prepare(q * 2 + 1, 1)
                prepare(q * 2 + 2, 0)
            prepare(NBLK - 2, 1)
            prepare(NBLK - 1, 0)

            def scores(s, par, c):
                n = s * CH + c
                if c == 0:
                    pe.wait_ge(xb_lo, s + 1)
                wait_for(pe, relu_done, n + 1 - since(c))
                for h in range(2):
                    t = 2 * c + h
                    dst = ps[:, S_BANK + c % 3, h * BW:(h + 1) * BW]
                    for k in range(KC):
                        hi, lo = (w_all[:, k, half, t * P:(t + 1) * P] for half in range(2))
                        nc.tensor.matmul(dst, hi, xb[:, 0, k, :], start=(k == 0), stop=False)
                        nc.tensor.matmul(dst, hi, xb[:, 1, k, :], start=False, stop=False)
                        last = nc.tensor.matmul(dst, lo, xb[:, 0, k, :], start=False, stop=(k == KC - 1))
                last.then_inc(scores_done, 1)

            def turn_max(s):
                pe.wait_ge(top2_ready, s + 1)
                for h in range(2):
                    last = nc.tensor.transpose(ps[:, TOP_BANK, h * P:(h + 1) * P], top2[:, h * P:(h + 1) * P], ident[:, :])
                last.then_inc(top_turned, 1)

            def spread_max(s):
                pe.wait_ge(diag_ready, s + 1)
                wait_for(pe, lowered, s * CH)
                nc.tensor.matmul(ps[:, MAX_BANK, 0:BW], ones[:, :], diag[:, :, :].rearrange("p h n -> p (h n)"), start=True,
                                 stop=True).then_inc(max_done, 1)

            def turn_sum(s):
                pe.wait_ge(total2_ready, s + 1)
                wait_for(pe, y_ready, s * 2)
                for h in range(2):
                    last = nc.tensor.transpose(ps[:, SUM_BANK, h * P:(h + 1) * P], total2[:, h * P:(h + 1) * P],
                                               ident[:, :])
                last.then_inc(sum_turned, 1)

            def attend(s, par, h, chunks):
                for c in chunks:
                    if h == 0:
                        pe.wait_ge(att_lo, s * CH + c + 1)
                    if c == 0:
                        wait_for(pe, y_ready, s * 2 + h - 1)
                    for u in range(2):
                        t = 2 * c + u
                        cols = slice(u * BW + h * P, u * BW + (h + 1) * P)
                        hi, lo = (att[:, par, c, half, cols] for half in range(2))
                        nc.tensor.matmul(ps[:, O_BANK + h, :], hi, V[:, t, 0, :], start=(t == 0), stop=False)
                        nc.tensor.matmul(ps[:, O_BANK + h, :], hi, V[:, t, 1, :], start=False, stop=False)
                        last = nc.tensor.matmul(ps[:, O_BANK + h, :], lo, V[:, t, 0, :], start=False, stop=(t == T - 1))
                if chunks[-1] == CH - 1:
                    last.then_inc(av_done, 1)

            def step(s, par, first=False):
                for c in range(CH):
                    if first and c == 2:
                        turn_max(s - 1)
                    if first and c == 3:
                        spread_max(s - 1)
                    scores(s, par, c)
                attend(s - 1, 1 - par, 0, range(0, 4))
                turn_max(s)
                attend(s - 1, 1 - par, 0, range(4, 7))
                spread_max(s)
                attend(s - 1, 1 - par, 0, range(7, 10))
                turn_sum(s - 1)
                attend(s - 1, 1 - par, 0, range(10, CH))
                attend(s - 1, 1 - par, 1, range(0, CH))

            pe.wait_ge(w_lo, NBLK)
            pe.wait_ge(v_lo, T)
            pe.wait_ge(b_ready, 1)
            pe.wait_ge(ident_ready, 1)
            for c in range(CH):
                scores(0, 0, c)
            step(1, 1, first=True)
            with pe.Fori(0, NBLK // 2 - 1) as q:
                step(q * 2 + 2, 0)
                step(q * 2 + 3, 1)
            step(NBLK - 1, 0)
            attend(NBLK - 1, 0, 0, range(0, CH))
            turn_sum(NBLK - 1)
            attend(NBLK - 1, 0, 1, range(0, CH))


def kernel(x, adj, L0_gnn_Wf, L0_gnn_bf, L0_gnn_Wg, L0_gnn_bg, L0_gnn_W, L0_gnn_bW):
    import numpy as np
    import concourse.bacc as bacc
    from concourse.bass_utils import run_bass_kernel_spmd

    x, adj = np.asarray(x), np.asarray(adj)
    n, d = x.shape
    blocks = -(-n // BW)
    padded = blocks * BW
    x_rows = np.zeros((padded, d), x.dtype)
    x_rows[:n] = x
    xT_blocks = x_rows.reshape(blocks, BW, d // P, P).transpose(0, 3, 2, 1).reshape(blocks, P, -1)
    adj_rows = np.zeros((padded, padded), adj.dtype)
    adj_rows[:n, :n] = adj
    adjT_blocks = adj_rows.reshape(blocks, BW, padded // P, P).transpose(0, 3, 2, 1).reshape(blocks, P, -1)

    def columns(w):
        return np.asarray(w).T.reshape(d // P, P, -1).transpose(1, 0, 2)

    arrays = {
        "x_rows": x_rows,
        "xT_blocks": xT_blocks,
        "adjT_blocks": adjT_blocks,
        "WfT": columns(L0_gnn_Wf),
        "bf_cols": np.asarray(L0_gnn_bf).reshape(d // P, P).T,
        "WgT": columns(L0_gnn_Wg),
        "bg_cols": np.asarray(L0_gnn_bg).reshape(d // P, P).T,
        "W": np.asarray(L0_gnn_W),
        "bW": np.asarray(L0_gnn_bW),
    }
    arrays = {name: np.ascontiguousarray(a) for name, a in arrays.items()}
    nc = bacc.Bacc("TRN2", target_bir_lowering=False, num_devices=1, dynamic_dma_scratch_size=1024)
    args = [nc.dram_tensor(name, a.shape, mybir.dt.from_np(a.dtype), kind="ExternalInput").ap()
            for name, a in arrays.items()]
    out = nc.dram_tensor("out", x_rows.shape, F32, kind="ExternalOutput").ap()
    gnn_kernel(nc, *args, out)
    r = run_bass_kernel_spmd(nc, [arrays], core_ids=[0])
    return r.results[0]["out"][:n]
```

```python
from contextlib import ExitStack

import concourse.bass as bass
from concourse import mybir

ALU = mybir.AluOpType
ACT = mybir.ActivationFunctionType
AX = mybir.AxisListType
F32 = mybir.dt.float32
F16 = mybir.dt.float16
BF16 = mybir.dt.bfloat16
I32 = mybir.dt.int32
RED_MAX = bass.bass_isa.ReduceOp.max

P = 128
BW = 2 * P
EPS = 1e-5
TOP = 14
PSCALE = float(2 ** TOP)
MASKED = -float(2.0 ** 126)
PAD_BIAS = -1e30
LEAST_MAX = float(2.0 ** -30)
EXPONENT_BITS = 0x7F800000
SCALE_BITS = float((TOP + 2 * 127) << 23)


def gnn_kernel(nc, x_rows, xT_blocks, adjT_blocks, WfT, bf_cols, WgT, bg_cols, W, bW, out):
    NP, D = x_rows.shape
    NBLK = xT_blocks.shape[0]
    KC = D // P
    T = NP // P
    CH = T // 2
    KD = KC * D
    assert NBLK == NP // BW == CH and NBLK % 2 == 1 and KC == 4
    EARLY = 8
    NORM_STEPS = 5
    XPIECES = [(0, 2), (2, 3), (3, 5), (5, 6), (6, 7), (7, 9), (9, 11), (11, 12), (12, NBLK)]

    with ExitStack() as ctx:
        def sb(name, shape, dt):
            return ctx.enter_context(nc.sbuf_tensor(name, shape, dt))

        def sem(name):
            return ctx.enter_context(nc.semaphore(name))

        w_all = sb("w_all", [P, KC, 2, NP], F16)
        V = sb("V", [P, T, 2, D], F16)
        x_all = V[:, :, :, :].rearrange("p t s d -> p (t s d)").bitcast(F32).rearrange("p (b n) -> p b n", b=NBLK)
        ident = sb("ident", [P, P], F32)
        ones = sb("ones", [P, P], F32)
        b_all = sb("b_all", [P, T], F32)
        Ws = sb("Ws", [P, KC, 2, D], F16)
        S = sb("S", [P, 2, CH, 2 * BW], F32)
        att = S[:, :, :, :].rearrange("p b c n -> p (b c n)").bitcast(F16).rearrange(
            "p (b c s n) -> p b c s n", b=2, c=CH, s=2)
        adj_t = sb("adj_t", [P, CH, 2 * BW], I32)
        penalty = sb("penalty", [P, 2, 2 * BW], BF16)
        late = sb("late", [P, 6 * BW + 2 * D], F32)
        E = late[:, 0:6 * BW].rearrange("p (c n) -> p c n", c=3)
        y = late[:, 6 * BW:].rearrange("p (h d) -> p h d", h=2)
        x32 = sb("x32", [P, KC, BW], F32)
        xb = sb("xb", [P, 2, KC, BW], F16)
        top = sb("top", [P, 2 * BW], F32)
        top2 = sb("top2", [P, BW], F32)
        total = sb("total", [P, 2 * BW], F32)
        total2 = sb("total2", [P, BW], F32)
        flat0 = S[:, 0, :, :].rearrange("p c n -> p (c n)")
        flat1 = S[:, 1, :, :].rearrange("p c n -> p (c n)")
        flat_adj = adj_t[:, :, :].rearrange("p c n -> p (c n)").bitcast(F32)
        WfT_n = flat_adj[:, 0:KD].rearrange("p (c d) -> p c d", c=KC)
        WgT_n = flat_adj[:, KD:2 * KD].rearrange("p (c d) -> p c d", c=KC)
        W_n = flat0[:, 0:KD].rearrange("p (c d) -> p c d", c=KC)
        z = flat0[:, KD:3 * KD].rearrange("p (s c d) -> p s c d", s=2, c=KC)
        B = late[:, 0:KD].bitcast(F16).rearrange("p (c s d) -> p c s d", c=KC, s=2)
        xp = flat1[:, 0:2 * KC * BW].bitcast(F16).rearrange("p (b s c n) -> p b s c n", b=2, s=2, c=KC)
        w32 = flat1[:, 2 * KC * BW:3 * KC * BW].rearrange("p (c n) -> p c n", c=KC)
        v32 = flat1[:, 3 * KC * BW:3 * KC * BW + 2 * D].rearrange("p (b d) -> p b d", b=2)
        bWs = flat1[:, 3 * KC * BW + 2 * D:3 * KC * BW + 3 * D]
        bf_c = sb("bf_c", [P, KC], F32)
        bg_c = sb("bg_c", [P, KC], F32)
        bb_c = sb("bb_c", [P, KC], F32)
        bb_1 = sb("bb_1", [P, 1], F32)
        c_col = sb("c_col", [P, KC], F32)
        cs_col = sb("cs_col", [P, KC], F32)
        vb32 = sb("vb32", [P, KC], F32)
        vb = sb("vb", [P, KC, 2], F16)
        b_sum = sb("b_sum", [P, 2], F32)
        prod_max = sb("prod_max", [P, KC + 1], F32)
        X_STATS = 4
        stats = sb("stats", [P, X_STATS + len(XPIECES)], F32)
        stats_all = sb("stats_all", [P, X_STATS + len(XPIECES)], F32)
        sc = sb("sc", [P, 29], F32)
        pad_bias = sb("pad_bias", [P, 1], F32)
        top_col = sb("top_col", [P, 2], F32)
        fin = sb("fin", [P, 2, 4], F32)
        RECIPROCAL, FACTOR, VARIANCE, RSTD = (slice(n, n + 1) for n in range(4))
        bn6 = sb("bn6", [P, 2, 6], F32)
        bn2 = sb("bn2", [P, 2, 2], F32)
        neg_half = sb("neg_half", [P, 1], F32)
        carrier = sb("carrier", [P, 2], F32)

        ps = ctx.enter_context(nc.psum_tensor("ps", [P, 8, 512], F32))
        S_BANK, O_BANK, TOP_BANK, MAX_BANK, SUM_BANK = 0, 3, 5, 6, 7
        PROD_BANK, W_BANK, V_BANK, B_BANK, SMALL_BANK, FIRST_BANK, LAST_BANK = 0, 0, 4, 6, 7, 7, 2

        wT_in = sem("wT_in")
        w_in = sem("w_in")
        biases_in = sem("biases_in")
        bW_in = sem("bW_in")
        x_in = [sem(f"x_in{n}") for n in range(len(XPIECES))]
        ident_zeroed = sem("ident_zeroed")
        ident_ready = sem("ident_ready")
        ones_ready = sem("ones_ready")
        half_ready = sem("half_ready")
        bb_ready = sem("bb_ready")
        z_scaled = sem("z_scaled")
        z_added = sem("z_added")
        product_done = sem("product_done")
        small_done = sem("small_done")
        prep = sem("prep")
        stats_ready = sem("stats_ready")
        stats_summed = sem("stats_summed")
        scales_ready = sem("scales_ready")
        W_scaled = sem("W_scaled")
        W_hi = sem("W_hi")
        W_ready = sem("W_ready")
        B_hi = sem("B_hi")
        B_ready = sem("B_ready")
        xp_hi = sem("xp_hi")
        xp_lo = sem("xp_lo")
        w_done = sem("w_done")
        w_f32 = sem("w_f32")
        w_hi = sem("w_hi")
        w_lo = sem("w_lo")
        v_done = sem("v_done")
        v_f32 = sem("v_f32")
        v_hi = sem("v_hi")
        v_lo = sem("v_lo")
        b_done = sem("b_done")
        b_copied = sem("b_copied")
        b_ready = sem("b_ready")
        adj_in = sem("adj_in")
        x32_in = sem("x32_in")
        xb_hi = sem("xb_hi")
        xb_lo = sem("xb_lo")
        y_in = sem("y_in")
        scores_done = sem("scores_done")
        relu_done = sem("relu_done")
        penalty_ready = sem("penalty_ready")
        masked = sem("masked")
        topped = sem("topped")
        top2_ready = sem("top2_ready")
        top_turned = sem("top_turned")
        top_col_ready = sem("top_col_ready")
        max_done = sem("max_done")
        lowered = sem("lowered")
        exp_done = sem("exp_done")
        att_hi = sem("att_hi")
        att_lo = sem("att_lo")
        summed = sem("summed")
        total2_ready = sem("total2_ready")
        sum_done = sem("sum_done")
        av_done = sem("av_done")
        norm = sem("norm")
        y_ready = sem("y_ready")
        rstd_ready = sem("rstd_ready")
        out_ready = sem("out_ready")
        stored = sem("stored")

        (mW, mB, mX, mX_first, mV, mw, sW, sX, sX_first, sB, sV, sw, exponent, _, iWX, _, iBX, _, ratio_v, _, ratio_w,
         _, ratio_b, _, wX, score_unit, beta, iV, out_unit) = range(29)

        def col(k, n=1):
            return sc[:, k:k + n]

        def own(k, b):
            return col(k + 1) if isinstance(b, int) and b < XPIECES[0][1] else col(k)

        def at(ap, k):
            return ap[:, k] if isinstance(k, int) else ap[:, bass.ds(k, 1)].squeeze(1)

        def wait_for(eng, signal, value):
            if not (isinstance(value, int) and value <= 0):
                eng.wait_ge(signal, value)

        def wait_apart(dve, signal, value, word):
            dve.wait_ge(signal, value)
            nc.vector.memset(carrier[:, word:word + 1], 0.0)

        def w_block(b, half):
            cols = slice(b * BW, (b + 1) * BW) if isinstance(b, int) else bass.ds(b * BW, BW)
            return w_all[:, :, half, cols]

        def turns(early):
            return [3, 4, 5, 6, 8, 9, 10, 11, 12] if early == 0 else range(0, 2 * (CH - early), 2)

        def since(c):
            return 3 if c >= 3 else CH - max(k for k in range(CH) if k % 3 == c % 3) + c

        block = ctx.enter_context(nc.Block())

        @block.sync
        def _(sp):
            sp.dma_start(WgT_n, WgT).then_inc(wT_in, 16)
            sp.dma_start(WfT_n, WfT).then_inc(wT_in, 16)
            sp.dma_start(bWs, bW.rearrange("(a d) -> a d", a=1).to_broadcast([P, D])).then_inc(bW_in, 16)
            sp.dma_start(W_n, W.rearrange("(c p) d -> p c d", p=P)).then_inc(w_in, 16)
            for n, (a, b) in enumerate(XPIECES):
                sp.dma_start(x_all[:, a:b, :], xT_blocks[a:b].rearrange("b p n -> p b n")).then_inc(x_in[n], 16)

            def load_adj(s):
                src = adjT_blocks[s] if isinstance(s, int) else adjT_blocks[bass.ds(s, 1)].squeeze(0)
                sp.dma_start(adj_t[:, :, :].rearrange("p c n -> p (c n)"), src).then_inc(adj_in, 16)

            def load_x32(s):
                src = xT_blocks[s] if isinstance(s, int) else xT_blocks[bass.ds(s, 1)].squeeze(0)
                sp.dma_start(x32[:, :, :].rearrange("p c n -> p (c n)"), src).then_inc(x32_in, 16)

            def rows(ap, s):
                r = ap[s * BW:(s + 1) * BW] if isinstance(s, int) else ap[bass.ds(s * BW, BW)]
                return r.rearrange("(h p) d -> p h d", p=P)

            load_x32(0)
            sp.wait_ge(product_done, KC)
            sp.wait_ge(small_done, 1)
            load_adj(0)

            def load_next(s):
                wait_for(sp, xb_lo, s)
                load_x32(s)
                sp.wait_ge(penalty_ready, s * CH)
                load_adj(s)

            def step(s, more):
                if not (isinstance(s, int) and s == 1):
                    sp.wait_ge(out_ready, (s - 1) * 2)
                    sp.dma_start(rows(out, s - 2), y[:, :, :]).then_inc(stored, 16)
                    sp.wait_ge(stored, (s - 1) * 16)
                sp.dma_start(y[:, :, :], rows(x_rows, s - 1)).then_inc(y_in, 16)
                if more:
                    load_next(s + 1)

            load_next(1)
            sp.wait_ge(w_done, NBLK)
            step(1, True)
            with sp.Fori(0, NBLK // 2 - 1) as q:
                step(q * 2 + 2, True)
                step(q * 2 + 3, True)
            step(NBLK - 1, False)
            sp.wait_ge(out_ready, 2 * (NBLK - 1))
            sp.dma_start(rows(out, NBLK - 2), y[:, :, :]).then_inc(stored, 16)
            sp.wait_ge(stored, 16 * (NBLK - 1))
            sp.dma_start(y[:, :, :], rows(x_rows, NBLK - 1)).then_inc(y_in, 16)
            for h in range(2):
                sp.wait_ge(out_ready, 2 * NBLK - 1 + h)
                sp.dma_start(rows(out, NBLK - 1)[:, h, :], y[:, h, :]).then_inc(stored, 16)
            sp.wait_ge(stored, 16 * (NBLK + 1))

        @block.gpsimd
        def _(pool):
            nc.gpsimd.memset(ident[:, :], 0.0).then_inc(ident_zeroed, 1)
            pool.wait_ge(ident_zeroed, 1)
            nc.gpsimd.affine_select(out=ident[:, :], in_=ident[:, :], compare_op=ALU.not_equal, fill=1.0, base=0,
                                    pattern=[[-1, P]], channel_multiplier=1).then_inc(ident_ready, 1)
            nc.gpsimd.memset(neg_half[:, :], -0.5).then_inc(half_ready, 1)
            pool.wait_ge(half_ready, 1)
            pool.wait_ge(ones_ready, 1)

            def all_max(n, a, b):
                pool.wait_ge(stats_ready, n + 1)
                nc.gpsimd.partition_all_reduce(stats_all[:, a:b], stats[:, a:b], P, RED_MAX).then_inc(stats_summed, 1)

            all_max(0, 0, 3)
            pool.wait_ge(z_scaled, 2)
            nc.gpsimd.tensor_tensor(z[:, :, 0:2, :], z[:, :, 0:2, :], z[:, :, 2:4, :], ALU.add).then_inc(z_added, 1)
            all_max(1, X_STATS, X_STATS + 1)
            pool.wait_ge(z_added, 1)
            nc.gpsimd.tensor_tensor(z[:, :, 0, :], z[:, :, 0, :], z[:, :, 1, :], ALU.add).then_inc(z_added, 1)
            pool.wait_ge(W_hi, 1)
            nc.gpsimd.tensor_tensor(Ws[:, :, 1, :], W_n, Ws[:, :, 0, :], ALU.subtract).then_inc(W_ready, 1)
            all_max(2, 1, 4)
            all_max(3, X_STATS, X_STATS + len(XPIECES))

            def sums(s, chunks):
                for c in chunks:
                    n = s * CH + c
                    pool.wait_ge(exp_done, n + 1)
                    if c == 0:
                        wait_for(pool, total2_ready, s)
                        nc.gpsimd.tensor_tensor(total[:, :].rearrange("p (a n) -> p a n", n=P),
                                                E[:, 0, :].rearrange("p (a n) -> p a n", n=P),
                                                ones[:, :].unsqueeze(1).to_broadcast([P, 2 * BW // P, P]),
                                                ALU.mult).then_inc(summed, 1)
                    else:
                        pool.wait_ge(summed, n)
                        nc.gpsimd.tensor_tensor(total[:, :], total[:, :], E[:, c % 3, :], ALU.add).then_inc(summed, 1)
                if chunks[-1] == CH - 1:
                    pool.wait_ge(summed, (s + 1) * CH)
                    wait_for(pool, sum_done, s)
                    nc.gpsimd.tensor_tensor(total2[:, :], total[:, 0:BW], total[:, BW:2 * BW],
                                            ALU.add).then_inc(total2_ready, 1)

            def rstd(s, h):
                pool.wait_ge(norm, (s * 2 + h + 1) * NORM_STEPS)
                nc.gpsimd.tensor_tensor(fin[:, h, RSTD], fin[:, h, VARIANCE], neg_half[:, :], ALU.pow).then_inc(rstd_ready, 1)

            def step(s, early):
                if early[0] > 0:
                    sums(s - 1, range(early[0], CH))
                rstd_first = early[1] // 2
                if rstd_first:
                    sums(s, range(0, rstd_first))
                rstd(s - 1, 0)
                if early[1] > rstd_first:
                    sums(s, range(rstd_first, early[1]))
                rstd(s - 1, 1)

            sums(0, range(0, CH))
            step(1, (0, EARLY))
            with pool.Fori(0, NBLK // 2 - 1) as q:
                step(q * 2 + 2, (EARLY, EARLY))
                step(q * 2 + 3, (EARLY, EARLY))
            step(NBLK - 1, (EARLY, CH))
            rstd(NBLK - 1, 0)
            rstd(NBLK - 1, 1)

        @block.scalar
        def _(act):
            act.dma_start(bf_c[:, :], bf_cols).then_inc(biases_in, 16)
            act.dma_start(bg_c[:, :], bg_cols).then_inc(biases_in, 16)
            act.wait_ge(biases_in, 32)
            act.wait_ge(wT_in, 32)
            for s, (w, b) in enumerate(((WfT_n, bg_c), (WgT_n, bf_c))):
                for c in range(KC):
                    last = nc.scalar.activation(z[:, s, c, :], w[:, c, :], ACT.Copy, scale=b[:, c:c + 1])
                last.then_inc(z_scaled, 1)
            act.wait_ge(w_in, 16)
            act.wait_ge(scales_ready, 1)
            nc.scalar.activation(W_n, W_n, ACT.Copy, scale=col(sW)).then_inc(W_scaled, 1)
            act.wait_ge(W_scaled, 1)
            nc.scalar.copy(Ws[:, :, 0, :], W_n).then_inc(W_hi, 1)

            def xp_split(b, par):
                wait_for(act, v_done, (b - 1) * 2)
                wait_for(act, w_done, b - 1)
                nc.scalar.activation(xp[:, par, 0, :, :].rearrange("p c n -> p (c n)"), at(x_all, b), ACT.Copy,
                                     scale=own(sX, b)).then_inc(xp_hi, 1)

            def w_split(b, par):
                act.wait_ge(w_done, b + 1)
                wait_for(act, w_lo, b)
                for m in range(KC):
                    last = nc.scalar.activation(w32[:, m, :], ps[:, W_BANK + 2 * par + m // 2, m % 2 * BW:(m % 2 + 1) * BW],
                                                ACT.Identity, bias=cs_col[:, m:m + 1], scale=own(ratio_w, b))
                last.then_inc(w_f32, 1)
                act.wait_ge(w_f32, b + 1)
                nc.scalar.copy(w_block(b, 0), w32).then_inc(w_hi, 1)

            def v_split(t, h):
                act.wait_ge(v_f32, t + 1)
                nc.scalar.copy(at(V, t)[:, 0, :], v32[:, h, :]).then_inc(v_hi, 1)

            def x_split(s):
                act.wait_ge(x32_in, s * 16 + 16)
                wait_for(act, scores_done, s * CH)
                nc.scalar.activation(xb[:, 0, :, :], x32[:, :, :], ACT.Copy, scale=col(sX)).then_inc(xb_hi, 1)

            def relu_first(c, bank=FIRST_BANK):
                act.wait_ge(b_ready, c + 1)
                act.wait_ge(scores_done, c + 1)
                for h in range(2):
                    last = nc.scalar.activation(at(S[:, 0, :, :], c)[:, h * BW:(h + 1) * BW],
                                                ps[:, bank, h * BW:(h + 1) * BW], ACT.Relu,
                                                bias=at(b_all.rearrange("p (t o) -> p t o", o=1), c * 2 + h))
                last.then_inc(relu_done, 1)

            act.wait_ge(scales_ready, 2)
            xp_split(0, 0)

            def prepare(b, par, more=True):
                if more:
                    xp_split(b + 1, 1 - par)
                w_split(b, par)
                v_split(b * 2, 0)
                v_split(b * 2 + 1, 1)
                relu_first(b - 1)

            act.wait_ge(scales_ready, 3)
            for c in range(KC):
                nc.scalar.activation(B[:, c, 0, :], ps[:, PROD_BANK + c, :], ACT.Copy, scale=col(sB)).then_inc(B_hi, 1)
            xp_split(1, 1)
            act.wait_ge(scales_ready, 4)
            x_split(0)
            v_split(0, 0)
            act.wait_ge(scales_ready, 5)
            w_split(0, 0)
            v_split(1, 1)
            prepare(1, 1)
            with act.Fori(0, NBLK // 2 - 1) as q:
                prepare(q * 2 + 2, 0)
                prepare(q * 2 + 3, 1)
            w_split(NBLK - 1, 0)
            relu_first(NBLK - 2)
            v_split(T - 2, 0)
            x_split(1)
            relu_first(NBLK - 1, LAST_BANK)

            def relu(s, par, c):
                act.wait_ge(scores_done, s * CH + c + 1)
                for h in range(2):
                    last = nc.scalar.activation(S[:, par, c, h * BW:(h + 1) * BW],
                                                ps[:, S_BANK + c % 3, h * BW:(h + 1) * BW], ACT.Relu,
                                                bias=b_all[:, 2 * c + h:2 * c + h + 1])
                last.then_inc(relu_done, 1)

            def soften(s, par, c):
                n = s * CH + c
                act.wait_ge(lowered, n + 1)
                wait_for(act, att_lo, n + 1 - since(c))
                wait_for(act, summed, n + 1 - since(c))
                if c < CH - 1:
                    last = nc.scalar.activation(E[:, c % 3, :], S[:, par, c, :], ACT.Exp, scale=col(score_unit))
                else:
                    nc.scalar.activation(E[:, c % 3, 0:BW], S[:, par, c, 0:BW], ACT.Exp, scale=col(score_unit))
                    last = nc.scalar.activation(E[:, c % 3, BW:2 * BW], S[:, par, c, BW:2 * BW], ACT.Exp,
                                                bias=pad_bias[:, :], scale=col(score_unit))
                last.then_inc(exp_done, 1)
                act.wait_ge(exp_done, n + 1)
                nc.scalar.activation(att[:, par, c, 0, :], E[:, c % 3, :], ACT.Copy, scale=PSCALE).then_inc(att_hi, 1)

            def step(s, par, early):
                left = list(range(early[0], CH))
                for c in range(CH):
                    relu(s, par, c)
                    if c - 1 in turns(early[0]):
                        soften(s - 1, 1 - par, left.pop(0))
                if early[1] < CH:
                    x_split(s + 1)
                for c in left:
                    soften(s - 1, 1 - par, c)
                for c in range(early[1]):
                    soften(s, par, c)

            v_split(T - 1, 1)
            step(1, 1, (0, EARLY))
            with act.Fori(0, NBLK // 2 - 1) as q:
                step(q * 2 + 2, 0, (EARLY, EARLY))
                step(q * 2 + 3, 1, (EARLY, EARLY))
            step(NBLK - 1, 0, (EARLY, CH))

        @block.vector
        def _(dve):
            done = [0]

            def link(ins):
                done[0] += 1
                ins.then_inc(prep, 1)
                dve.wait_ge(prep, done[0])

            def amax(dst, src):
                return nc.vector.tensor_reduce(dst, src, AX.X if len(src.shape) == 2 else AX.XY, ALU.max,
                                               apply_absolute_value=True)

            def scale_of(dst, maxima, n=1):
                exponents = col(exponent, n).bitcast(I32)
                link(nc.vector.tensor_scalar(exponents, maxima.bitcast(I32), EXPONENT_BITS, None, ALU.bitwise_and))
                return nc.vector.tensor_scalar(dst.bitcast(I32), exponents, -1.0, SCALE_BITS, ALU.mult, ALU.add)

            nc.vector.memset(ones[:, :], 1.0).then_inc(ones_ready, 1)
            dve.wait_ge(biases_in, 32)
            link(nc.vector.tensor_tensor(bb_c[:, :], bf_c[:, :], bg_c[:, :], ALU.mult))
            nc.vector.tensor_reduce(bb_1[:, :], bb_c[:, :], AX.X, ALU.add).then_inc(bb_ready, 1)
            nc.vector.memset(stats[:, 1:2], 0.0)
            dve.wait_ge(bW_in, 16)
            amax(stats[:, 2:3], bWs)
            dve.wait_ge(w_in, 16)
            amax(stats[:, 0:1], W_n).then_inc(stats_ready, 1)

            def x_max(n):
                a, b = XPIECES[n]
                dve.wait_ge(x_in[n], 16)
                return amax(stats[:, X_STATS + n:X_STATS + n + 1], x_all[:, a:b, :])

            def product_max(m):
                dve.wait_ge(product_done, m + 1)
                amax(prod_max[:, m:m + 1], ps[:, PROD_BANK + m, :])

            def xp_lo_part(b, par):
                dve.wait_ge(xp_hi, b + 1)
                nc.vector.scalar_tensor_tensor(xp[:, par, 1, :, :].rearrange("p c n -> p (c n)"), at(x_all, b), own(sX, b),
                                               xp[:, par, 0, :, :].rearrange("p c n -> p (c n)"), ALU.mult,
                                               ALU.subtract).then_inc(xp_lo, 1)

            def v_from(b, h):
                t = b * 2 + h
                dve.wait_ge(v_done, t + 1)
                wait_for(dve, v_hi, t - 1)
                nc.vector.scalar_tensor_tensor(v32[:, h, :], ps[:, V_BANK + h, :], own(ratio_v, b), bWs, ALU.mult,
                                               ALU.add).then_inc(v_f32, 1)

            def v_lo_part(b, h):
                t = b * 2 + h
                dve.wait_ge(v_hi, t + 1)
                nc.vector.tensor_tensor(at(V, t)[:, 1, :], v32[:, h, :], at(V, t)[:, 0, :], ALU.subtract).then_inc(v_lo, 1)

            def b_copy(b):
                parts = ps[:, B_BANK, 0:4].rearrange("p (h s) -> p h s", h=2)
                dve.wait_ge(b_done, b + 1)
                wait_for(dve, b_ready, b)
                nc.vector.tensor_reduce(b_sum[:, :], parts, AX.X, ALU.add).then_inc(b_copied, 1)

            def b_from(b):
                dve.wait_ge(b_copied, b + 1)
                nc.vector.tensor_scalar(at(b_all.rearrange("p (b h) -> p b h", h=2), b), b_sum[:, :], own(ratio_b, b),
                                        col(beta), ALU.mult, ALU.add).then_inc(b_ready, 1)

            dve.wait_ge(stats_summed, 1)
            link(nc.vector.tensor_scalar(col(mW), stats_all[:, 0:1], LEAST_MAX, None, ALU.max))
            scale_of(col(sW), col(mW)).then_inc(scales_ready, 1)
            x_max(0).then_inc(stats_ready, 1)
            x_max(1)
            dve.wait_ge(stats_summed, 2)
            link(nc.vector.tensor_scalar(col(mX_first), stats_all[:, X_STATS:X_STATS + 1], LEAST_MAX, None, ALU.max))
            scale_of(col(sX_first), col(mX_first)).then_inc(scales_ready, 1)
            dve.wait_ge(scales_ready, 2)
            product_max(0)
            x_max(2)
            product_max(1)
            xp_lo_part(0, 0)
            product_max(2)
            product_max(3)
            dve.wait_ge(small_done, 1)
            amax(stats[:, 3:4], ps[:, SMALL_BANK, 0:KC])
            amax(prod_max[:, KC:KC + 1], ps[:, SMALL_BANK, KC:2 * KC])
            nc.vector.tensor_copy(c_col[:, :], ps[:, SMALL_BANK, 0:KC])
            nc.vector.tensor_copy(vb32[:, :], ps[:, SMALL_BANK, KC:2 * KC])
            link(nc.vector.tensor_copy(col(beta), ps[:, SMALL_BANK, 2 * KC:2 * KC + 1]))
            nc.vector.tensor_reduce(stats[:, 1:2], prod_max[:, :], AX.X, ALU.max).then_inc(stats_ready, 1)
            x_max(3)
            dve.wait_ge(stats_summed, 3)
            link(nc.vector.tensor_scalar(col(mB), stats_all[:, 1:2], LEAST_MAX, None, ALU.max))
            scale_of(col(sB), col(mB)).then_inc(scales_ready, 1)
            x_max(4)
            for c in range(KC):
                dve.wait_ge(B_hi, c + 1)
                last = nc.vector.scalar_tensor_tensor(B[:, c, 1, :], ps[:, PROD_BANK + c, :], col(sB), B[:, c, 0, :],
                                                      ALU.mult, ALU.subtract)
            last.then_inc(B_ready, 1)
            link(nc.vector.tensor_scalar(vb32[:, :], vb32[:, :], col(sB), None, ALU.mult))
            link(nc.vector.tensor_copy(vb[:, :, 0], vb32[:, :]))
            nc.vector.tensor_tensor(vb[:, :, 1], vb32[:, :], vb[:, :, 0], ALU.subtract).then_inc(B_ready, 1)
            xp_lo_part(1, 1)
            x_max(5)
            b_copy(0)
            for n in range(6, len(XPIECES)):
                last = x_max(n)
            last.then_inc(stats_ready, 1)
            dve.wait_ge(stats_summed, 4)
            link(nc.vector.tensor_reduce(col(mX), stats_all[:, X_STATS:], AX.X, ALU.max))
            link(nc.vector.tensor_scalar(col(mX), col(mX), LEAST_MAX, None, ALU.max))
            scale_of(col(sX), col(mX)).then_inc(scales_ready, 1)
            dve.wait_ge(scales_ready, 4)
            link(nc.vector.tensor_scalar(col(mV, 2), col(mW, 2), col(mX), float(D), ALU.mult, ALU.mult))
            link(nc.vector.tensor_tensor(col(mV, 2), col(mV, 2), stats_all[:, 2:4], ALU.add))
            link(scale_of(col(sV, 2), col(mV, 2), 2))
            nc.vector.tensor_scalar(bWs, bWs, col(sV), None, ALU.mult)
            link(nc.vector.tensor_scalar(col(iWX, 2), col(sX, 2), col(sW), None, ALU.mult))
            link(nc.vector.reciprocal(col(iWX, 2), col(iWX, 2)))
            link(nc.vector.tensor_scalar(col(ratio_v, 2), col(iWX, 2), col(sV), None, ALU.mult))
            v_from(0, 0)
            nc.vector.tensor_scalar(cs_col[:, :], c_col[:, :], col(sw), None, ALU.mult)
            link(nc.vector.tensor_scalar(col(iBX, 2), col(sX, 2), col(sB), None, ALU.mult))
            link(nc.vector.reciprocal(col(iBX, 2), col(iBX, 2)))
            nc.vector.tensor_scalar(col(ratio_w, 2), col(iBX, 2), col(sw), None, ALU.mult).then_inc(scales_ready, 1)
            v_lo_part(0, 0)
            v_from(0, 1)
            link(nc.vector.tensor_tensor(col(wX), col(sw), col(sX), ALU.mult))
            nc.vector.reciprocal(col(score_unit), col(wX))
            nc.vector.tensor_scalar(col(ratio_b, 2), col(iBX, 2), col(wX), None, ALU.mult)
            nc.vector.tensor_tensor(col(beta), col(beta), col(wX), ALU.mult)
            link(nc.vector.reciprocal(col(iV), col(sV)))
            nc.vector.tensor_scalar(col(out_unit), col(iV), 1.0 / PSCALE, None, ALU.mult)
            dve.wait_ge(ident_ready, 1)
            link(nc.vector.tensor_scalar(pad_bias[:, :], ident[:, P - 1:P], PAD_BIAS, None, ALU.mult))

            def v_both(b):
                for h in range(2):
                    v_from(b, h)
                    v_lo_part(b, h)

            def w_lo_part(b):
                dve.wait_ge(w_hi, b + 1)
                nc.vector.tensor_tensor(w_block(b, 1), w32, w_block(b, 0), ALU.subtract).then_inc(w_lo, 1)

            def x_split(s):
                dve.wait_ge(xb_hi, s + 1)
                nc.vector.scalar_tensor_tensor(xb[:, 1, :, :].rearrange("p c n -> p (c n)"),
                                               x32[:, :, :].rearrange("p c n -> p (c n)"), col(sX),
                                               xb[:, 0, :, :].rearrange("p c n -> p (c n)"), ALU.mult,
                                               ALU.subtract).then_inc(xb_lo, 1)

            def mask(s, par, c, slot, first=False):
                n = s * CH + c
                chunk = at(S[:, par, :, :], c)
                nc.vector.tensor_scalar(penalty[:, slot, :], at(adj_t, c), 0.0, MASKED, ALU.is_le,
                                        ALU.mult).then_inc(penalty_ready, 1)
                dve.wait_ge(relu_done, n + 1)
                dve.wait_ge(penalty_ready, n + 1)
                nc.vector.tensor_tensor(chunk, chunk, penalty[:, slot, :], ALU.add).then_inc(masked, 1)
                dve.wait_ge(masked, n + 1)
                if first:
                    nc.vector.tensor_copy(top[:, :], chunk).then_inc(topped, 1)
                else:
                    dve.wait_ge(topped, n)
                    nc.vector.tensor_tensor(top[:, :], top[:, :], chunk, ALU.max).then_inc(topped, 1)

            def max_over_tiles(s):
                dve.wait_ge(topped, (s + 1) * CH)
                nc.vector.tensor_tensor(top2[:, :], top[:, 0:BW], top[:, BW:2 * BW], ALU.max).then_inc(top2_ready, 1)

            def max_over_partitions(s):
                dve.wait_ge(top_turned, s + 1)
                wait_for(dve, max_done, s)
                nc.vector.tensor_reduce(top_col[:, :], ps[:, TOP_BANK, 0:BW].rearrange("p (h n) -> p h n", h=2), AX.X,
                                        ALU.max).then_inc(top_col_ready, 1)

            def lower(s, par, c):
                if c == 0:
                    dve.wait_ge(max_done, s + 1)
                chunk = S[:, par, c, :].rearrange("p (h n) -> p h n", h=2)
                nc.vector.tensor_tensor(chunk, chunk, ps[:, MAX_BANK, 0:BW].unsqueeze(1).to_broadcast([P, 2, BW]),
                                        ALU.subtract).then_inc(lowered, 1)

            def att_lo_part(s, par, c):
                dve.wait_ge(att_hi, s * CH + c + 1)
                nc.vector.scalar_tensor_tensor(att[:, par, c, 1, :], E[:, c % 3, :], PSCALE, att[:, par, c, 0, :],
                                               ALU.mult, ALU.subtract).then_inc(att_lo, 1)

            def finish(s, h):
                t = s * 2 + h
                k = t * NORM_STEPS
                f = fin[:, h, :]
                if h == 0:
                    dve.wait_ge(sum_done, s + 1)
                nc.vector.reciprocal(f[:, RECIPROCAL], ps[:, SUM_BANK, h:h + 1]).then_inc(norm, 1)
                dve.wait_ge(norm, k + 1)
                nc.vector.tensor_scalar(f[:, FACTOR], f[:, RECIPROCAL], col(out_unit), None, ALU.mult).then_inc(norm, 1)
                dve.wait_ge(norm, k + 2)
                dve.wait_ge(av_done, t + 1)
                dve.wait_ge(y_in, s * 16 + 16)
                nc.vector.scalar_tensor_tensor(y[:, h, :], ps[:, O_BANK + h, :], f[:, FACTOR], y[:, h, :], ALU.mult,
                                               ALU.add).then_inc(y_ready, 1)
                dve.wait_ge(y_ready, t + 1)
                nc.vector.bn_stats(bn6[:, h, :], y[:, h, :]).then_inc(norm, 1)
                wait_apart(dve, norm, k + 3, h)
                nc.vector.bn_aggr(bn2[:, h, :], bn6[:, h, :]).then_inc(norm, 1)
                dve.wait_ge(norm, k + 4)
                nc.vector.tensor_scalar(f[:, VARIANCE], bn2[:, h, 1:2], EPS, None, ALU.add).then_inc(norm, 1)
                dve.wait_ge(rstd_ready, t + 1)
                nc.vector.tensor_scalar(y[:, h, :], y[:, h, :], bn2[:, h, 0:1], f[:, RSTD], ALU.subtract,
                                        ALU.mult).then_inc(out_ready, 1)

            def soften(s, par, chunks):
                chunks = list(chunks)
                if not chunks:
                    return
                lower(s, par, chunks[0])
                for c in chunks[1:]:
                    lower(s, par, c)
                    att_lo_part(s, par, c - 1)
                att_lo_part(s, par, chunks[-1])

            def step(s, par, early):
                left = list(range(early[0], CH))
                ahead = []

                def soften_next():
                    if left:
                        lower(s - 1, 1 - par, left[0])
                    if ahead:
                        att_lo_part(s - 1, 1 - par, ahead.pop())
                    if left:
                        ahead.append(left.pop(0))

                if early[0] == 0:
                    max_over_partitions(s - 1)
                dve.wait_ge(adj_in, s * 16 + 16)
                for c in range(CH):
                    mask(s, par, c, (par + c) % 2, c == 0)
                    if c in turns(early[0]):
                        soften_next()
                max_over_tiles(s)
                if early[1] < CH:
                    x_split(s + 1)
                for _ in range(2):
                    soften_next()
                max_over_partitions(s)
                while left or ahead:
                    soften_next()
                soften(s, par, range(0, early[1] // 2))
                finish(s - 1, 0)
                soften(s, par, range(early[1] // 2, early[1]))
                finish(s - 1, 1)

            def prepare(b, par):
                xp_lo_part(b + 1, 1 - par)
                w_lo_part(b)
                b_copy(b)
                b_from(b)
                v_both(b)
                mask(0, 0, b - 1, 1 - par, isinstance(b, int) and b == 1)

            x_split(0)
            w_lo_part(0)
            v_lo_part(0, 1)
            b_from(0)
            dve.wait_ge(adj_in, 16)
            prepare(1, 1)
            with dve.Fori(0, NBLK // 2 - 1) as q:
                prepare(q * 2 + 2, 0)
                prepare(q * 2 + 3, 1)
            w_lo_part(NBLK - 1)
            b_copy(NBLK - 1)
            b_from(NBLK - 1)
            mask(0, 0, NBLK - 2, 1)
            v_from(NBLK - 1, 0)
            v_lo_part(NBLK - 1, 0)
            x_split(1)
            mask(0, 0, NBLK - 1, 0)
            max_over_tiles(0)
            v_from(NBLK - 1, 1)
            v_lo_part(NBLK - 1, 1)
            step(1, 1, (0, EARLY))
            with dve.Fori(0, NBLK // 2 - 1) as q:
                step(q * 2 + 2, 0, (EARLY, EARLY))
                step(q * 2 + 3, 1, (EARLY, EARLY))
            step(NBLK - 1, 0, (EARLY, CH))
            finish(NBLK - 1, 0)
            finish(NBLK - 1, 1)

        @block.tensor
        def _(pe):
            pe.wait_ge(wT_in, 32)
            for m in range(KC):
                for k in range(KC):
                    last = nc.tensor.matmul(ps[:, PROD_BANK + m, :], WgT_n[:, k, m * P:(m + 1) * P], WfT_n[:, k, :],
                                            start=(k == 0), stop=(k == KC - 1))
                last.then_inc(product_done, 1)
            pe.wait_ge(ones_ready, 1)
            pe.wait_ge(z_added, 2)
            for s in range(2):
                for m in range(KC):
                    nc.tensor.matmul(ps[:, SMALL_BANK, s * KC + m:s * KC + m + 1], z[:, s, 0, m * P:(m + 1) * P],
                                     ones[:, 0:1], start=True, stop=True)
            pe.wait_ge(bb_ready, 1)
            nc.tensor.matmul(ps[:, SMALL_BANK, 2 * KC:2 * KC + 1], ones[:, :], bb_1[:, :], start=True,
                             stop=True).then_inc(small_done, 1)

            def w_of(b, par):
                wait_for(pe, w_f32, b - 1)
                for m in range(KC):
                    dst = ps[:, W_BANK + 2 * par + m // 2, m % 2 * BW:(m % 2 + 1) * BW]
                    for k in range(KC):
                        hi, lo = (B[:, k, s, m * P:(m + 1) * P] for s in range(2))
                        nc.tensor.matmul(dst, hi, xp[:, par, 0, k, :], start=(k == 0), stop=False)
                        nc.tensor.matmul(dst, hi, xp[:, par, 1, k, :], start=False, stop=False)
                        last = nc.tensor.matmul(dst, lo, xp[:, par, 0, k, :], start=False, stop=(k == KC - 1))
                last.then_inc(w_done, 1)

            def v_of(b, par, h):
                wait_for(pe, v_f32, b * 2 + h - 1)
                for k in range(KC):
                    hi, lo = (xp[:, par, s, k, h * P:(h + 1) * P] for s in range(2))
                    nc.tensor.matmul(ps[:, V_BANK + h, :], hi, Ws[:, k, 0, :], start=(k == 0), stop=False)
                    nc.tensor.matmul(ps[:, V_BANK + h, :], hi, Ws[:, k, 1, :], start=False, stop=False)
                    last = nc.tensor.matmul(ps[:, V_BANK + h, :], lo, Ws[:, k, 0, :], start=False, stop=(k == KC - 1))
                last.then_inc(v_done, 1)

            def b_of(b, par):
                wait_for(pe, b_copied, b)
                for h in range(2):
                    for k in range(KC):
                        hi, lo = (xp[:, par, s, k, h * P:(h + 1) * P] for s in range(2))
                        nc.tensor.matmul(ps[:, B_BANK, 2 * h:2 * h + 2], hi, vb[:, k, :], start=(k == 0), stop=False)
                        last = nc.tensor.matmul(ps[:, B_BANK, 2 * h:2 * h + 1], lo, vb[:, k, 0:1], start=False,
                                                stop=(k == KC - 1))
                last.then_inc(b_done, 1)

            def scores_chunk(dst, c):
                for h in range(2):
                    start = c * BW + h * P
                    cols = slice(start, start + P) if isinstance(c, int) else bass.ds(start, P)
                    to = dst[:, h * BW:(h + 1) * BW]
                    for k in range(KC):
                        hi, lo = (w_all[:, k, half, cols] for half in range(2))
                        nc.tensor.matmul(to, hi, xb[:, 0, k, :], start=(k == 0), stop=False)
                        nc.tensor.matmul(to, hi, xb[:, 1, k, :], start=False, stop=False)
                        last = nc.tensor.matmul(to, lo, xb[:, 0, k, :], start=False, stop=(k == KC - 1))
                last.then_inc(scores_done, 1)

            def scores_first(c, bank=FIRST_BANK):
                pe.wait_ge(w_lo, c + 1)
                if isinstance(c, int) and c == 0:
                    pe.wait_ge(xb_lo, 1)
                wait_for(pe, relu_done, c if bank == FIRST_BANK else c - 1)
                scores_chunk(ps[:, bank, :], c)

            def prepare(b, par):
                pe.wait_ge(xp_lo, b + 1)
                w_of(b, par)
                b_of(b, par)
                v_of(b, par, 0)
                v_of(b, par, 1)
                scores_first(b - 1)

            pe.wait_ge(W_ready, 1)
            pe.wait_ge(xp_lo, 1)
            v_of(0, 0, 0)
            v_of(0, 0, 1)
            pe.wait_ge(B_ready, 2)
            b_of(0, 0)
            w_of(0, 0)
            prepare(1, 1)
            with pe.Fori(0, NBLK // 2 - 1) as q:
                prepare(q * 2 + 2, 0)
                prepare(q * 2 + 3, 1)
            pe.wait_ge(xp_lo, NBLK)
            w_of(NBLK - 1, 0)
            b_of(NBLK - 1, 0)
            scores_first(NBLK - 2)
            v_of(NBLK - 1, 0, 0)
            scores_first(NBLK - 1, LAST_BANK)
            v_of(NBLK - 1, 0, 1)

            def scores(s, par, c):
                n = s * CH + c
                if c == 0:
                    pe.wait_ge(xb_lo, s + 1)
                wait_for(pe, relu_done, n + 1 - since(c))
                scores_chunk(ps[:, S_BANK + c % 3, :], c)

            def turn_max(s):
                pe.wait_ge(top2_ready, s + 1)
                for h in range(2):
                    last = nc.tensor.transpose(ps[:, TOP_BANK, h * P:(h + 1) * P], top2[:, h * P:(h + 1) * P], ident[:, :])
                last.then_inc(top_turned, 1)

            def spread_max(s):
                pe.wait_ge(top_col_ready, s + 1)
                wait_for(pe, lowered, s * CH)
                for h in range(2):
                    last = nc.tensor.transpose(ps[:, MAX_BANK, h * P:(h + 1) * P], top_col[:, h:h + 1].to_broadcast([P, P]),
                                               ident[:, :])
                last.then_inc(max_done, 1)

            def add_sum(s):
                pe.wait_ge(total2_ready, s + 1)
                wait_for(pe, y_ready, s * 2)
                for h in range(2):
                    last = nc.tensor.matmul(ps[:, SUM_BANK, h:h + 1], total2[:, h * P:(h + 1) * P], ones[:, 0:1],
                                            start=True, stop=True)
                last.then_inc(sum_done, 1)

            def attend(s, par, h, chunks):
                for c in chunks:
                    if h == 0:
                        pe.wait_ge(att_lo, s * CH + c + 1)
                    if c == 0:
                        wait_for(pe, y_ready, s * 2 + h - 1)
                    for u in range(2):
                        t = 2 * c + u
                        cols = slice(u * BW + h * P, u * BW + (h + 1) * P)
                        hi, lo = (att[:, par, c, half, cols] for half in range(2))
                        nc.tensor.matmul(ps[:, O_BANK + h, :], hi, V[:, t, 0, :], start=(t == 0), stop=False)
                        nc.tensor.matmul(ps[:, O_BANK + h, :], hi, V[:, t, 1, :], start=False, stop=False)
                        last = nc.tensor.matmul(ps[:, O_BANK + h, :], lo, V[:, t, 0, :], start=False, stop=(t == T - 1))
                if CH - 1 in chunks:
                    last.then_inc(av_done, 1)

            def step(s, par, first=False):
                for c in range(CH):
                    if first and c == 2:
                        pe.wait_ge(v_lo, T)
                        turn_max(s - 1)
                    if first and c == 3:
                        spread_max(s - 1)
                    scores(s, par, c)
                turn, spread, add = (7, 11, CH) if first else (4, 7, 10)
                attend(s - 1, 1 - par, 0, range(0, turn))
                turn_max(s)
                attend(s - 1, 1 - par, 0, range(turn, spread))
                spread_max(s)
                attend(s - 1, 1 - par, 0, range(spread, add))
                add_sum(s - 1)
                attend(s - 1, 1 - par, 0, range(add, CH))
                attend(s - 1, 1 - par, 1, range(0, CH))

            pe.wait_ge(ident_ready, 1)
            step(1, 1, first=True)
            with pe.Fori(0, NBLK // 2 - 1) as q:
                step(q * 2 + 2, 0)
                step(q * 2 + 3, 1)
            step(NBLK - 1, 0)
            attend(NBLK - 1, 0, 0, range(0, CH))
            add_sum(NBLK - 1)
            attend(NBLK - 1, 0, 1, range(0, CH))


def kernel(x, adj, L0_gnn_Wf, L0_gnn_bf, L0_gnn_Wg, L0_gnn_bg, L0_gnn_W, L0_gnn_bW):
    import numpy as np
    import concourse.bacc as bacc
    from concourse.bass_utils import run_bass_kernel_spmd

    x, adj = np.asarray(x), np.asarray(adj)
    n, d = x.shape
    blocks = -(-n // BW)
    padded = blocks * BW
    assert padded - n == 1
    x_rows = np.zeros((padded, d), x.dtype)
    x_rows[:n] = x
    xT_blocks = x_rows.reshape(blocks, BW, d // P, P).transpose(0, 3, 2, 1).reshape(blocks, P, -1)
    adj_rows = np.zeros((padded, padded), adj.dtype)
    adj_rows[:n, :n] = adj
    adjT_blocks = adj_rows.reshape(blocks, BW, padded // P, P).transpose(0, 3, 2, 1).reshape(blocks, P, -1)

    def columns(w):
        return np.asarray(w).T.reshape(d // P, P, -1).transpose(1, 0, 2)

    arrays = {
        "x_rows": x_rows,
        "xT_blocks": xT_blocks,
        "adjT_blocks": adjT_blocks,
        "WfT": columns(L0_gnn_Wf),
        "bf_cols": np.asarray(L0_gnn_bf).reshape(d // P, P).T,
        "WgT": columns(L0_gnn_Wg),
        "bg_cols": np.asarray(L0_gnn_bg).reshape(d // P, P).T,
        "W": np.asarray(L0_gnn_W),
        "bW": np.asarray(L0_gnn_bW),
    }
    arrays = {name: np.ascontiguousarray(a) for name, a in arrays.items()}
    nc = bacc.Bacc("TRN2", target_bir_lowering=False, num_devices=1, dynamic_dma_scratch_size=1024)
    args = [nc.dram_tensor(name, a.shape, mybir.dt.from_np(a.dtype), kind="ExternalInput").ap()
            for name, a in arrays.items()]
    out = nc.dram_tensor("out", x_rows.shape, F32, kind="ExternalOutput").ap()
    gnn_kernel(nc, *args, out)
    r = run_bass_kernel_spmd(nc, [arrays], core_ids=[0])
    return r.results[0]["out"][:n]
```
